# Optimizing a Trainium2 kernel written in Bass

```python
import numpy as np
import jax
import jax.numpy as jnp

def _softmax(x, axis=-1):
    return jax.nn.softmax(x, axis=axis)

def _gelu(x):
    return jax.nn.gelu(x, approximate=True)

def _silu(x):
    return jax.nn.silu(x)

def _sigmoid(x):
    return jax.nn.sigmoid(x)

def _layernorm(x, axis=-1, eps=1e-05):
    m = jnp.mean(x, axis=axis, keepdims=True)
    v = jnp.var(x, axis=axis, keepdims=True)
    return (x - m) / jnp.sqrt(v + eps)

def _scatter_add(tgt, idx, src, axis=0):
    return tgt.at[idx].add(src)

def _segment_sum(src, seg, n):
    return jax.ops.segment_sum(src, seg, n)
kernel_name = 'mk_xattn_seq_d1_seqx_r4_669047'

def setup_inputs(seed: int=0):
    np.random.seed(seed)
    _w = jnp.asarray

    def _rec_inputs():
        import jax
        import jax.numpy as jnp
        _rk = jax.random.key(seed)
        x = -0.000719 + 1.001 * jax.random.normal(jax.random.fold_in(_rk, 1), (32, 256, 320), jnp.float32)
        _lenS = 256 - jax.random.randint(jax.random.fold_in(_rk, 7), (32,), 0, max(1, 256 // 4) + 1, jnp.int32)
        _lenS2 = 120 - jax.random.randint(jax.random.fold_in(_rk, 8), (32,), 0, max(1, 120 // 4) + 1, jnp.int32)
        _ctx_2048P = jax.random.normal(jax.random.fold_in(_rk, 11), (32, 16, 512), jnp.float32)
        _ctx_2048c = jax.random.dirichlet(jax.random.fold_in(_rk, 511), 0.3 * jnp.ones((16,), jnp.float32), (32, 120))
        _ctx_2048t = jnp.einsum('bsk,bkd->bsd', _ctx_2048c, _ctx_2048P)
        _ctx_2048t = _ctx_2048t * jax.lax.rsqrt(jnp.mean(jnp.square(_ctx_2048t)) + 1e-12) * 0.953939
        ctx_2048 = 0.00257118 + 0.99863 * (_ctx_2048t + 0.3 * jax.random.normal(jax.random.fold_in(_rk, 611), (32, 120, 512), jnp.float32))
        fside_S_0 = jax.random.uniform(jax.random.fold_in(_rk, 12), (256,), jnp.float32, 0.0, 0.999706)
        return (x, ctx_2048, fside_S_0)
    x, ctx_2048, fside_S_0 = _rec_inputs()

    def _L0_xattn_setup():
        import jax, jax.numpy as jnp
        import numpy as np
        HEADS = 20
        NUM_TOKENS = 4
        IP_SCALE = 1.0
        SEM_SCALE = 0.5
        RESCALE = 1.0
        EPS = 1e-12

        def _l2norm(x, axis=-1):
            n = jnp.sqrt(jnp.sum(x * x, axis=axis, keepdims=True))
            return x / jnp.maximum(n, EPS)
        key = jax.random.key(seed)
        ks = jax.random.split(key, 10)
        B, S, C = (2, 256, 320)
        T, E = (81, 512)
        inp = {'hidden_states': jax.random.normal(ks[0], (B, S, C), jnp.float32), 'encoder_hidden_states': jax.random.normal(ks[1], (B, T, E), jnp.float32), 'spatial_mask': jax.random.uniform(ks[2], (S,), jnp.float32), 'W_q': jax.random.normal(ks[3], (C, C), jnp.float32) * C ** (-0.5), 'W_k': jax.random.normal(ks[4], (E, C), jnp.float32) * E ** (-0.5), 'W_v': jax.random.normal(ks[5], (E, C), jnp.float32) * E ** (-0.5), 'W_k_ip': jax.random.normal(ks[6], (E, C), jnp.float32) * E ** (-0.5), 'W_v_ip': jax.random.normal(ks[7], (E, C), jnp.float32) * E ** (-0.5), 'W_out': jax.random.normal(ks[8], (C, C), jnp.float32) * C ** (-0.5), 'b_out': jnp.zeros((C,), jnp.float32)}
        return inp
    _L0_xattn_all = _L0_xattn_setup()
    _L0_xattn_in = {k: v for k, v in _L0_xattn_all.items() if k in ('W_q', 'W_k', 'W_v', 'W_k_ip', 'W_v_ip', 'W_out', 'b_out')}
    del _L0_xattn_all
    return {'x': x, 'ctx_2048': ctx_2048, 'fside_S_0': fside_S_0, 'L0_xattn_W_q': _L0_xattn_in['W_q'], 'L0_xattn_W_k': _L0_xattn_in['W_k'], 'L0_xattn_W_v': _L0_xattn_in['W_v'], 'L0_xattn_W_k_ip': _L0_xattn_in['W_k_ip'], 'L0_xattn_W_v_ip': _L0_xattn_in['W_v_ip'], 'L0_xattn_W_out': _L0_xattn_in['W_out'], 'L0_xattn_b_out': _L0_xattn_in['b_out']}

def reference(x, ctx_2048, fside_S_0, L0_xattn_W_q, L0_xattn_W_k, L0_xattn_W_v, L0_xattn_W_k_ip, L0_xattn_W_v_ip, L0_xattn_W_out, L0_xattn_b_out):
    import jax
    import jax.numpy as jnp

    def _L0_xattn_ref(hidden_states, encoder_hidden_states, spatial_mask, W_q, W_k, W_v, W_k_ip, W_v_ip, W_out, b_out):
        import jax, jax.numpy as jnp
        import numpy as np
        HEADS = 20
        NUM_TOKENS = 4
        IP_SCALE = 1.0
        SEM_SCALE = 0.5
        RESCALE = 1.0
        EPS = 1e-12

        def _l2norm(x, axis=-1):
            n = jnp.sqrt(jnp.sum(x * x, axis=axis, keepdims=True))
            return x / jnp.maximum(n, EPS)
        B, S, C = hidden_states.shape
        H = HEADS
        Dh = C // H
        attn_scale = Dh ** (-0.5)
        residual = hidden_states
        text_ehs = encoder_hidden_states[:, :-NUM_TOKENS]
        ip_ehs = encoder_hidden_states[:, -NUM_TOKENS:]

        def heads(x):
            return x.reshape(B, -1, H, Dh).transpose(0, 2, 1, 3)
        q = heads(hidden_states @ W_q)
        k_t = heads(text_ehs @ W_k)
        v_t = heads(text_ehs @ W_v)
        scores_t = jnp.einsum('bhsd,bhtd->bhst', q, k_t) * attn_scale
        probs_t = jax.nn.softmax(scores_t, axis=-1)
        text_out = jnp.einsum('bhst,bhtd->bhsd', probs_t, v_t)
        text_out = text_out.transpose(0, 2, 1, 3).reshape(B, S, C)
        k_ip = heads(ip_ehs @ W_k_ip)
        v_ip = heads(ip_ehs @ W_v_ip)
        attn_scores = jnp.einsum('bhsd,bhnd->bhsn', q, k_ip) * attn_scale
        qsem = jnp.einsum('bhst,bte->bhse', probs_t, text_ehs)
        qsem = _l2norm(qsem)
        ip_n = _l2norm(ip_ehs)
        sem = jnp.einsum('bhse,bne->bhsn', qsem, ip_n)
        sem = jax.lax.stop_gradient(sem)
        fused = attn_scores + SEM_SCALE * sem
        probs_ip = jax.nn.softmax(fused, axis=-1)
        probs_ip = probs_ip * spatial_mask[None, None, :, None]
        ip_out = jnp.einsum('bhsn,bhnd->bhsd', probs_ip, v_ip)
        ip_out = ip_out.transpose(0, 2, 1, 3).reshape(B, S, C)
        out = text_out + IP_SCALE * ip_out
        out = out @ W_out + b_out
        out = out + residual
        return out / RESCALE
    x = _L0_xattn_ref(x, ctx_2048, fside_S_0, L0_xattn_W_q, L0_xattn_W_k, L0_xattn_W_v, L0_xattn_W_k_ip, L0_xattn_W_v_ip, L0_xattn_W_out, L0_xattn_b_out)
    return x

_drawn_inputs = setup_inputs


def setup_inputs(seed=0):
    import zlib

    import numpy as np

    out = dict(_drawn_inputs(seed))
    spreads = {'L0_xattn_b_out': (0.0, 0.1)}
    factors = {}
    for name, (base, spread) in spreads.items():
        noise = np.random.default_rng([zlib.crc32(name.encode()), seed]).standard_normal(out[name].shape)
        drawn = base * np.exp(spread * noise) if base else spread * noise
        out[name] = jnp.asarray(drawn.astype(out[name].dtype))
    for name, factor in factors.items():
        out[name] = (out[name] * factor).astype(out[name].dtype)
    return out
```

```python
import concourse.bass as bass
from concourse import mybir
from contextlib import ExitStack

B, S, C = 32, 256, 320
T_ALL, E = 120, 512
N_IP = 4
T = T_ALL - N_IP
H = 20
DH = C // H
SCALE = DH ** -0.5
SEM_SCALE = 0.5
EPS = 1e-12
P = 128
QB = S // P
KC, KE = 3, E // P
ROWS = [P, P, C - 2 * P]
HU = 4
UNITS = H // HU * QB
ALL = B * UNITS
ZW = N_IP + 2 + DH
BLK = ZW + T + ZW
YW = ZW + T
TH = T // 4
FRONT = 5
BACK = 5


def cross_attention(nc, x, xt01, xt2, ctxt, ipt, mask, wq, wk, wv, wki, wvi, wo, bo,
                    ident_c, headmask_c, ipmask_c, out):
    f32 = mybir.dt.float32
    ALU = mybir.AluOpType
    ACT = mybir.ActivationFunctionType
    AX = mybir.AxisListType.X

    ctx = ExitStack()
    with ctx:
        def sb(name, shape, dt=f32):
            return ctx.enter_context(nc.sbuf_tensor(name, shape, dt))

        def ps(name, shape):
            return ctx.enter_context(nc.psum_tensor(name, shape, f32))

        def sem(name):
            return ctx.enter_context(nc.semaphore(name))

        Wq, Wo = sb("Wq", [P, KC, C]), sb("Wo", [P, KC, C])
        Wk, Wv = sb("Wk", [P, KE, C]), sb("Wv", [P, KE, C])
        Wki, Wvi = sb("Wki", [P, KE, C]), sb("Wvi", [P, KE, C])
        ident, ones = sb("ident", [P, P]), sb("ones", [P, P])
        headmask = sb("headmask", [P, P // DH])
        ipmask = sb("ipmask", [H * N_IP, C])
        smask = sb("smask", [P, QB])
        expo = sb("expo", [P, 1])
        scale_c = sb("scale_c", [P, 1])
        ipT, ipT2 = sb("ipT", [P, KE, B * N_IP]), sb("ipT2", [P, KE, B * N_IP])
        ipinv = sb("ipinv", [P, B * N_IP])
        kipT = sb("kipT", [P, KC, B * N_IP])
        vip = sb("vip", [B * N_IP, C])
        xT = [sb(f"xT{i}", [P, KC, S]) for i in range(2)]
        cT = [sb(f"cT{i}", [P, KE, T_ALL]) for i in range(2)]
        xn = [sb(f"xn{i}", [P, QB, C]) for i in range(2)]
        viprep = [sb(f"viprep{i}", [H * N_IP, C]) for i in range(2)]
        qT = [sb(f"qT{i}", [P, KC, S]) for i in range(2)]
        kT = [sb(f"kT{i}", [P, KC, T]) for i in range(2)]
        kbd = [sb(f"kbd{i}", [P, H, T_ALL]) for i in range(2)]
        rhs = [sb(f"rhs{i}", [T, H // 2, BLK]) for i in range(2)]
        vbd = [sb(f"vbd{i}", [H * N_IP, C]) for i in range(2)]
        rowmax = sb("rowmax", [P, 2, HU])
        shifted = sb("shifted", [P, 2, HU, T_ALL])
        prob = sb("prob", [P, 4, HU, T])
        probT = sb("probT", [T, 2, HU, P])
        yp = sb("yp", [P, 2, HU, T])
        half1 = sb("half1", [P, HU, T // 2])
        yq = [sb(f"yq{i}", [P, QB * H, TH]) for i in range(2)]
        zlo = [sb(f"zlo{i}", [P, QB * H, ZW]) for i in range(2)]
        sip = [sb(f"sip{i}", [P, QB * H, N_IP]) for i in range(2)]
        norm2, floor2, norm2c, rnorm, rl = (sb(n, [P, QB * H]) for n in
                                            ("norm2", "floor2", "norm2c", "rnorm", "rl"))
        cosn = sb("cosn", [P, QB * H, N_IP])
        fused = sb("fused", [P, QB * H, N_IP])
        fmax, fsum, frec, fscale = (sb(n, [P, QB * H]) for n in ("fmax", "fsum", "frec", "fscale"))
        fsh = sb("fsh", [P, QB * H, N_IP])
        fexp = sb("fexp", [P, QB * H, N_IP])
        pip = [sb(f"pip{i}", [P, QB, H * N_IP]) for i in range(2)]
        on = [sb(f"on{i}", [P, QB, C]) for i in range(2)]
        pipT = sb("pipT", [H * N_IP, S])
        oT = sb("oT", [P, KC, S])
        y = [sb(f"y{i}", [P, QB, C]) for i in range(2)]

        scoresP = [ps(f"scoresP{i}", [P, 512]) for i in range(2)]
        transP = ps("transP", [P, 512])
        sharedP = ps("sharedP", [P, 512])
        yP = [ps(f"yP{i}", [P, 2, 512]) for i in range(2)]

        vip_dram = nc.dram_tensor("vip_scratch", (B, N_IP, C), f32, kind="Internal").ap()

        weights_in, consts_in, vip_out = sem("weights_in"), sem("consts_in"), sem("vip_out")
        batch_in = [sem(f"batch_in{i}") for i in range(2)]
        xn_in = [sem(f"xn_in{i}") for i in range(2)]
        vip_in = [sem(f"vip_in{i}") for i in range(2)]
        stored = [sem(f"stored{i}") for i in range(2)]
        preset, expo_set, ip_squared = sem("preset"), sem("expo_set"), sem("ip_squared")
        ip_norm_mm, ip_k_mm, ip_v_mm = sem("ip_norm_mm"), sem("ip_k_mm"), sem("ip_v_mm")
        ip_floor, ip_inv, kip_ready, vip_ready = (sem("ip_floor"), sem("ip_inv"), sem("kip_ready"),
                                                  sem("vip_ready"))
        scores_mm, max_done, shift_done, exp_done = (sem("scores_mm"), sem("max_done"),
                                                     sem("shift_done"), sem("exp_done"))
        trans_mm, probT_ready, y_mm, yp_done, zlo_done = (sem("trans_mm"), sem("probT_ready"),
                                                          sem("y_mm"), sem("yp_done"), sem("zlo_done"))
        sip_done, half1_done, yq_done = sem("sip_done"), sem("half1_done"), sem("yq_done")
        front_mm, front_free = sem("front_mm"), sem("front_free")
        back_mm, back_free = sem("back_mm"), sem("back_free")
        g_copied, kbd_ready, vbd_ready = sem("g_copied"), sem("kbd_ready"), sem("vbd_ready")
        norm2_done, floor_done, rl_done, norm2c_done, rnorm_done, on_done = (
            sem("norm2_done"), sem("floor_done"), sem("rl_done"), sem("norm2c_done"),
            sem("rnorm_done"), sem("on_done"))
        cos_done, fused_done, fmax_done, fsh_done, fexp_done = (
            sem("cos_done"), sem("fused_done"), sem("fmax_done"), sem("fsh_done"), sem("fexp_done"))
        fsum_done, frec_done, fscale_done, pip_done = (sem("fsum_done"), sem("frec_done"),
                                                       sem("fscale_done"), sem("pip_done"))

        block = ctx.enter_context(nc.Block())

        N_WEIGHTS = 16 * 10
        N_CONSTS = 16 * 4

        def wait(eng, s, n):
            if not isinstance(n, int) or n > 0:
                eng.wait_ge(s, n)

        def is_unit(b, u):
            return not isinstance(b, int) or 0 <= UNITS * b + u < ALL

        def is_batch(b):
            return not isinstance(b, int) or 0 <= b < B

        def every_batch(eng, batch):
            for b in (-1, 0, 1):
                batch(b, b % 2, b // 2)
            with eng.Fori(1, B // 2 - 1) as i:
                for par in range(2):
                    batch(i * 2 + par, par, i)
            for b in (B - 2, B - 1, B, B + 1):
                batch(b, b % 2, b // 2)

        def slot(u):
            u %= UNITS
            return slice(u % QB * H + u // QB * HU, u % QB * H + u // QB * HU + HU)

        @block.sync
        def _(sp):
            sp.dma_start(ipT[:], ipt).then_inc(weights_in, 16)
            sp.dma_start(Wki[:], wki.rearrange("(k p) n -> p k n", p=P)).then_inc(weights_in, 16)
            sp.dma_start(Wvi[:], wvi.rearrange("(k p) n -> p k n", p=P)).then_inc(weights_in, 16)
            for w, src in ((Wq, wq), (Wo, wo)):
                sp.dma_start(w[:, 0:2, :], src[0:2 * P, :].rearrange("(k p) n -> p k n", p=P)).then_inc(
                    weights_in, 16)
                sp.dma_start(w[0:ROWS[2], 2, :], src[2 * P:C, :]).then_inc(weights_in, 16)
            sp.dma_start(Wo[ROWS[2]:ROWS[2] + 1, 2, :], bo).then_inc(weights_in, 16)
            sp.dma_start(Wk[:], wk.rearrange("(k p) n -> p k n", p=P)).then_inc(weights_in, 16)
            sp.dma_start(Wv[:], wv.rearrange("(k p) n -> p k n", p=P)).then_inc(weights_in, 16)

            def load_batch(b, par):
                sp.dma_start(xT[par][:, 0:2, :], xt01[b]).then_inc(batch_in[par], 16)
                sp.dma_start(xT[par][0:ROWS[2], 2, :], xt2[b]).then_inc(batch_in[par], 16)
                sp.dma_start(cT[par][:], ctxt[b]).then_inc(batch_in[par], 16)

            load_batch(0, 0)
            sp.wait_ge(vip_ready, 1)
            sp.dma_start(vip_dram.rearrange("b n c -> (b n) c"), vip[:]).then_inc(vip_out, 16)
            sp.wait_ge(vip_out, 16)

            def batch(b, par, pair):
                if is_batch(b + 2):
                    wait(sp, front_mm, FRONT * (b + 1))
                    load_batch(b + 2, par)
                if is_batch(b):
                    wait(sp, vbd_ready, b - 1)
                    sp.dma_start(viprep[par][:], vip_dram[b].unsqueeze(0).broadcast_to(
                        [H, N_IP, C])).then_inc(vip_in[par], 16)
                    wait(sp, back_free, BACK * (b - 1))
                    sp.dma_start(xn[par][:], x[b].rearrange("(q p) c -> p q c", p=P)).then_inc(
                        xn_in[par], 16)
                if is_batch(b - 2):
                    wait(sp, back_free, BACK * (b - 1))
                    sp.dma_start(out[b - 2].rearrange("(q p) c -> p q c", p=P), y[par][:]).then_inc(
                        stored[par], 16)

            every_batch(sp, batch)
            for par in range(2):
                sp.wait_ge(stored[par], 16 * (B // 2))

        @block.tensor
        def _(pe):
            mm, tr = nc.tensor.matmul, nc.tensor.transpose

            pe.wait_ge(preset, 1)
            pe.wait_ge(ip_squared, 1)
            for k in range(KE):
                last = mm(transP[:, 0:B * N_IP], ones[:], ipT2[:, k, :], start=k == 0, stop=k == KE - 1)
            last.then_inc(ip_norm_mm, 1)
            pe.wait_ge(weights_in, N_WEIGHTS)
            for m in range(KC):
                for k in range(KE):
                    last = mm(sharedP[0:ROWS[m], m * P:(m + 1) * P], Wki[:, k, m * P:m * P + ROWS[m]],
                              ipT[:, k, :], start=k == 0, stop=k == KE - 1)
            last.then_inc(ip_k_mm, 1)
            for k in range(KE):
                last = mm(scoresP[0][:, 0:C], ipT[:, k, :], Wvi[:, k, :], start=k == 0, stop=k == KE - 1)
            last.then_inc(ip_v_mm, 1)
            pe.wait_ge(consts_in, N_CONSTS)
            pe.wait_ge(kip_ready, 1)
            pe.wait_ge(vip_ready, 1)
            pe.wait_ge(ip_floor, 1)

            def front(b, par, pair, piece):
                if not is_batch(b):
                    return
                if piece == 0:
                    pe.wait_ge(batch_in[par], 48 * (pair + 1))
                    wait(pe, back_free, BACK * (b - 3) + 3)
                wait(pe, front_free, FRONT * b + piece)
                if piece == 0:
                    for m in range(2):
                        for k in range(KC):
                            last = mm(sharedP[:, m * S:(m + 1) * S], Wq[0:ROWS[k], k, m * P:(m + 1) * P],
                                      xT[par][0:ROWS[k], k, :], start=k == 0, stop=k == KC - 1)
                elif piece == 1:
                    for k in range(KC):
                        last = mm(sharedP[0:ROWS[2], 0:S], Wq[0:ROWS[k], k, 2 * P:C],
                                  xT[par][0:ROWS[k], k, :], start=k == 0, stop=k == KC - 1)
                elif piece == 2:
                    for m in range(KC):
                        for k in range(KE):
                            last = mm(sharedP[0:ROWS[m], m * T:(m + 1) * T],
                                      Wk[:, k, m * P:m * P + ROWS[m]], cT[par][:, k, 0:T],
                                      start=k == 0, stop=k == KE - 1)
                elif piece == 3:
                    for k in range(KE):
                        last = mm(sharedP[0:T, 0:C], cT[par][:, k, 0:T], Wv[:, k, :],
                                  start=k == 0, stop=k == KE - 1)
                else:
                    for k in range(KE):
                        last = mm(sharedP[0:T, 0:T_ALL], cT[par][:, k, 0:T], cT[par][:, k, :],
                                  start=k == 0, stop=k == KE - 1)
                last.then_inc(front_mm, 1)

            def back(b, par, pair, piece):
                if not is_batch(b):
                    return
                if piece in (0, 3):
                    n = b + 3 if piece == 0 else b + 4
                    pe.wait_ge(front_free, FRONT * (min(n, B) if isinstance(n, int) else n))
                if piece == 0:
                    pe.wait_ge(pip_done, b + 1)
                wait(pe, back_free, BACK * b + piece)
                if piece == 0:
                    for q in range(QB):
                        last = tr(sharedP[0:H * N_IP, q * P:(q + 1) * P], pip[par][:, q, :], ident[:])
                elif piece in (1, 2):
                    if piece == 1:
                        pe.wait_ge(on_done, b + 1)
                        pe.wait_ge(vbd_ready, b + 1)
                    tiles = (0, 1) if piece == 1 else (2,)
                    for m in tiles:
                        mm(sharedP[0:ROWS[m], m % 2 * S:m % 2 * S + S], vbd[par][:, m * P:m * P + ROWS[m]],
                           pipT[:], start=m == tiles[0], stop=False, skip_group_check=True)
                    for m in tiles:
                        for q in range(QB):
                            at = m % 2 * S + q * P
                            last = mm(sharedP[0:ROWS[m], at:at + P], on[par][:, q, m * P:m * P + ROWS[m]],
                                      ident[:], start=False, stop=True, is_transpose=True,
                                      skip_group_check=True)
                else:
                    q = piece - 3
                    for m in range(KC):
                        rows = ROWS[m] + (m == KC - 1)
                        last = mm(sharedP[:, 0:C], oT[0:rows, m, q * P:(q + 1) * P], Wo[0:rows, m, :],
                                  start=m == 0, stop=m == KC - 1)
                last.then_inc(back_mm, 1)

            def scores(b, par, u):
                if not is_unit(b, u):
                    return
                g, q = u // QB, u % QB
                m = g // 2
                if u == 0:
                    pe.wait_ge(kbd_ready, b + 1)
                    pe.wait_ge(front_free, FRONT * b + 2)
                wait(pe, shift_done, UNITS * b + u - 1)
                mm(scoresP[u % 2][:, 0:HU * T_ALL], qT[par][0:ROWS[m], m, q * P:(q + 1) * P],
                   kbd[par][0:ROWS[m], g * HU:(g + 1) * HU, :], start=True, stop=True).then_inc(scores_mm, 1)

            def transposes(b, par, u):
                if not is_unit(b, u):
                    return
                pe.wait_ge(exp_done, UNITS * b + u + 1)
                wait(pe, probT_ready, UNITS * b + u)
                for h in range(HU):
                    last = tr(transP[0:T, h * P:(h + 1) * P], prob[:, (2 * par + u) % 4, h, :], ident[:])
                last.then_inc(trans_mm, 1)

            def products(b, par, u):
                if not is_unit(b, u):
                    return
                if u == 0:
                    pe.wait_ge(front_free, FRONT * (b + 1))
                pe.wait_ge(probT_ready, UNITS * b + u + 1)
                wait(pe, yp_done, UNITS * b + u - 1)
                wait(pe, zlo_done, UNITS * b + u - 1)
                for h in range(HU):
                    r = h % 2
                    last = mm(yP[u % 2][:, h // 2, r * YW:(r + 1) * YW], probT[:, u % 2, h, :],
                              rhs[par][:, u // QB * 2 + h // 2, r * ZW:r * ZW + YW], start=True, stop=True)
                last.then_inc(y_mm, 1)

            SLOTS = {(0, 0): (back, -2, 0), (0, 1): (back, -2, 1), (1, 0): (back, -2, 2),
                     (1, 1): (front, 1, 0), (2, 0): (front, 1, 1), (2, 1): (front, 1, 2),
                     (3, 0): (front, 1, 3), (3, 1): (front, 1, 4),
                     (4, 1): (back, -2, 3), (5, 1): (back, -2, 4)}

            def batch(b, par, pair):
                def shared(u, k):
                    if (u, k) in SLOTS:
                        what, off, piece = SLOTS[u, k]
                        what(b + off, (par + off) % 2, pair + (par + off) // 2, piece)

                for u in range(UNITS):
                    shared(u, 0)
                    if u + 2 < UNITS:
                        scores(b, par, u + 2)
                    else:
                        scores(b + 1, 1 - par, u + 2 - UNITS)
                    transposes(b, par, u)
                    shared(u, 1)
                    if u:
                        products(b, par, u - 1)
                    else:
                        products(b - 1, 1 - par, UNITS - 1)

            every_batch(pe, batch)

        @block.scalar
        def _(act):
            copy = nc.scalar.copy
            act.dma_start(ident[:], ident_c).then_inc(consts_in, 16)
            act.dma_start(headmask[:], headmask_c).then_inc(consts_in, 16)
            act.dma_start(ipmask[:], ipmask_c).then_inc(consts_in, 16)
            act.dma_start(smask[:], mask).then_inc(consts_in, 16)

            act.wait_ge(ip_k_mm, 1)
            act.wait_ge(preset, 1)
            copy(kipT[:, 0:2, :], sharedP[:, 0:2 * P].rearrange("p (m n) -> p m n", m=2))
            copy(kipT[0:ROWS[2], 2, :], sharedP[0:ROWS[2], 2 * P:3 * P]).then_inc(kip_ready, 1)
            act.wait_ge(ip_v_mm, 1)
            copy(vip[:], scoresP[0][:, 0:C]).then_inc(vip_ready, 1)

            def front(b, par, pair, piece):
                if not is_batch(b):
                    return
                act.wait_ge(front_mm, FRONT * b + piece + 1)
                if piece == 0:
                    wait(act, scores_mm, UNITS * (b - 1))
                    copy(qT[par][:, 0:2, :], sharedP[:, 0:2 * S].rearrange("p (m s) -> p m s", m=2)
                         ).then_inc(front_free, 1)
                elif piece == 1:
                    copy(qT[par][0:ROWS[2], 2, :], sharedP[0:ROWS[2], 0:S]).then_inc(front_free, 1)
                elif piece == 2:
                    wait(act, kbd_ready, b - 1)
                    copy(kT[par][:, 0:2, :], sharedP[:, 0:2 * T].rearrange("p (m t) -> p m t", m=2))
                    copy(kT[par][0:ROWS[2], 2, :], sharedP[0:ROWS[2], 2 * T:3 * T]).then_inc(front_free, 1)
                elif piece == 3:
                    wait(act, y_mm, UNITS * (b - 1))
                    for r in range(2):
                        at = r * YW + ZW - DH
                        last = copy(rhs[par][:, :, at:at + DH],
                                    sharedP[0:T, 0:C].rearrange("p (j r d) -> p r j d", r=2, d=DH)[:, r])
                    last.then_inc(front_free, 1)
                else:
                    copy(rhs[par][:, :, ZW:YW], sharedP[0:T, 0:T].unsqueeze(1).broadcast_to(
                        [T, H // 2, T])).then_inc(g_copied, 1)

            def back(b, par, pair, piece):
                if not is_batch(b):
                    return
                act.wait_ge(back_mm, BACK * b + piece + 1)
                if piece == 0:
                    copy(pipT[:], sharedP[0:H * N_IP, 0:S]).then_inc(back_free, 1)
                elif piece == 1:
                    copy(oT[:, 0:2, :], sharedP[:, 0:2 * S].rearrange("p (m s) -> p m s", m=2)
                         ).then_inc(back_free, 1)
                else:
                    copy(oT[0:ROWS[2], 2, :], sharedP[0:ROWS[2], 0:S]).then_inc(back_free, 1)

            def evac_trans(b, par, u):
                if not is_unit(b, u):
                    return
                act.wait_ge(trans_mm, UNITS * b + u + 1)
                wait(act, y_mm, UNITS * b + u - 1)
                copy(probT[:, u % 2, :, :], transP[0:T, :].rearrange("t (h s) -> t h s", h=HU)
                     ).then_inc(probT_ready, 1)

            def exp_unit(b, par, u):
                if not is_unit(b, u):
                    return
                act.wait_ge(shift_done, UNITS * b + u + 1)
                wait(act, yp_done, UNITS * b + u - 3)
                nc.scalar.activation(prob[:, (2 * par + u) % 4, :, :], shifted[:, u % 2, :, 0:T], ACT.Exp,
                                     scale=SCALE).then_inc(exp_done, 1)

            def evac_zlo(b, par, u):
                if not is_unit(b, u):
                    return
                act.wait_ge(yp_done, UNITS * b + u + 1)
                if u == 0:
                    wait(act, cos_done, b - 1)
                    wait(act, on_done, b - 1)
                z = yP[u % 2][:, :, 0:2 * YW]
                for r in range(2):
                    at = r * (YW + T)
                    dst = zlo[par][:, slot(u), :].rearrange("p (k r) z -> p r k z", r=2)[:, r]
                    last = copy(dst, z[:, :, at:at + ZW])
                last.then_inc(zlo_done, 1)

            SLOTS = {(0, 0): (back, -2, 0), (0, 1): (back, -2, 1), (1, 0): (back, -2, 2),
                     (1, 1): (front, 1, 0), (2, 0): (front, 1, 1), (2, 1): (front, 1, 2),
                     (3, 0): (front, 1, 3), (3, 1): (front, 1, 4)}

            def batch(b, par, pair):
                def shared(u, k):
                    if (u, k) in SLOTS:
                        what, off, piece = SLOTS[u, k]
                        what(b + off, (par + off) % 2, pair + (par + off) // 2, piece)

                for u in range(UNITS):
                    shared(u, 0)
                    evac_trans(b, par, u)
                    shared(u, 1)
                    if u + 1 < UNITS:
                        exp_unit(b, par, u + 1)
                    else:
                        exp_unit(b + 1, 1 - par, 0)
                    if u >= 2:
                        evac_zlo(b, par, u - 2)
                    else:
                        evac_zlo(b - 1, 1 - par, u - 2 + UNITS)
                    if u == 8 and is_batch(b - 1):
                        act.wait_ge(fsh_done, b)
                        wait(act, pip_done, b - 1)
                        nc.scalar.activation(fexp[:], fsh[:], ACT.Exp).then_inc(fexp_done, 1)

            every_batch(act, batch)

        @block.vector
        def _(dve):
            v = nc.vector
            v.memset(ones[:], 1.0)
            for i in range(2):
                v.memset(rhs[i][:], 0.0)
            v.memset(oT[:], 1.0).then_inc(preset, 1)
            dve.wait_ge(preset, 1)
            for i in range(2):
                for r in range(2):
                    at = r * (YW + 0) + N_IP
                    v.memset(rhs[i][:, :, at:at + 1], 1.0)
            dve.wait_ge(weights_in, N_WEIGHTS)
            v.tensor_tensor(ipT2[:], ipT[:], ipT[:], ALU.mult).then_inc(ip_squared, 1)
            dve.wait_ge(ip_norm_mm, 1)
            v.tensor_scalar(ipinv[:], transP[:, 0:B * N_IP], EPS * EPS, 1.0 / SEM_SCALE ** 2,
                            ALU.max, ALU.mult).then_inc(ip_floor, 1)
            dve.wait_ge(consts_in, N_CONSTS)

            def softmax_shift(b, par, u):
                if not is_unit(b, u):
                    return
                sc = scoresP[u % 2][:, 0:HU * T_ALL].rearrange("p (h t) -> p h t", h=HU)
                dve.wait_ge(scores_mm, UNITS * b + u + 1)
                v.tensor_reduce(rowmax[:, u % 2, :], sc[:, :, 0:T], AX, ALU.max).then_inc(max_done, 1)
                dve.wait_ge(max_done, UNITS * b + u + 1)
                wait(dve, exp_done, UNITS * b + u - 1)
                wait(dve, sip_done, UNITS * b + u - 1)
                v.tensor_tensor(shifted[:, u % 2, :, :], sc, rowmax[:, u % 2, :].unsqueeze(2).broadcast_to(
                    [P, HU, T_ALL]), ALU.subtract).then_inc(shift_done, 1)

            def y_times_p(b, par, u):
                if not is_unit(b, u):
                    return
                dve.wait_ge(y_mm, UNITS * b + u + 1)
                wait(dve, half1_done, UNITS * b + u - 1)
                yv = yP[u % 2][:, :, ZW:ZW + 2 * T].rearrange("p k (r t) -> p k r t", r=2)
                v.tensor_tensor(yp[:, u % 2, :, :].rearrange("p (k r) t -> p k r t", r=2), yv,
                                prob[:, (2 * par + u) % 4, :, :].rearrange("p (k r) t -> p k r t", r=2),
                                ALU.mult).then_inc(yp_done, 1)

            def z_columns(b, par):
                if not is_batch(b):
                    return
                dve.wait_ge(g_copied, b + 1)
                if isinstance(b, int) and b == 0:
                    dve.wait_ge(ip_inv, 1)
                for r in range(2):
                    at = r * YW
                    last = v.tensor_tensor(
                        rhs[par][:, :, at:at + N_IP],
                        sharedP[0:T, T:T_ALL].unsqueeze(1).broadcast_to([T, H // 2, N_IP]),
                        ipinv[0:T, bass.ds(b * N_IP, N_IP)].unsqueeze(1).broadcast_to([T, H // 2, N_IP]),
                        ALU.mult)
                last.then_inc(front_free, 1)

            def norms(b, par):
                if not is_batch(b):
                    return
                dve.wait_ge(yq_done, UNITS * (b + 1))
                dve.wait_ge(zlo_done, UNITS * (b + 1))
                z = zlo[par]
                v.tensor_reduce(norm2[:], yq[par][:], AX, ALU.add).then_inc(norm2_done, 1)
                v.scalar_tensor_tensor(floor2[:], z[:, :, N_IP], EPS * EPS, z[:, :, N_IP], ALU.mult,
                                       ALU.mult).then_inc(floor_done, 1)
                v.reciprocal(rl[:], z[:, :, N_IP]).then_inc(rl_done, 1)
                dve.wait_ge(norm2_done, b + 1)
                dve.wait_ge(floor_done, b + 1)
                wait(dve, rnorm_done, b)
                v.tensor_tensor(norm2c[:], norm2[:], floor2[:], ALU.max).then_inc(norm2c_done, 1)
                dve.wait_ge(rl_done, b + 1)
                wait(dve, back_mm, BACK * (b - 1))
                v.tensor_tensor(on[par][:].rearrange("p q (h d) -> p (q h) d", d=DH), z[:, :, ZW - DH:ZW],
                                rl[:].unsqueeze(2).broadcast_to([P, QB * H, DH]), ALU.mult).then_inc(on_done, 1)

            def per_head(t):
                return t[:].unsqueeze(2).broadcast_to([P, QB * H, N_IP])

            def ip_scores(b, par):
                if not is_batch(b):
                    return
                dve.wait_ge(rnorm_done, b + 1)
                v.tensor_tensor(cosn[:], zlo[par][:, :, 0:N_IP], per_head(rnorm), ALU.mult).then_inc(cos_done, 1)
                dve.wait_ge(cos_done, b + 1)
                dve.wait_ge(sip_done, UNITS * (b + 1))
                v.tensor_tensor(fused[:], sip[par][:], cosn[:], ALU.add).then_inc(fused_done, 1)
                dve.wait_ge(fused_done, b + 1)
                v.tensor_reduce(fmax[:], fused[:], AX, ALU.max).then_inc(fmax_done, 1)
                dve.wait_ge(fmax_done, b + 1)
                wait(dve, fexp_done, b)
                v.tensor_tensor(fsh[:], fused[:], per_head(fmax), ALU.subtract).then_inc(fsh_done, 1)

            def ip_probs(b, par):
                if not is_batch(b):
                    return
                dve.wait_ge(fexp_done, b + 1)
                v.tensor_reduce(fsum[:], fexp[:], AX, ALU.add).then_inc(fsum_done, 1)
                dve.wait_ge(fsum_done, b + 1)
                v.reciprocal(frec[:], fsum[:]).then_inc(frec_done, 1)
                dve.wait_ge(frec_done, b + 1)
                v.tensor_tensor(fscale[:].rearrange("p (q h) -> p q h", q=QB),
                                frec[:].rearrange("p (q h) -> p q h", q=QB),
                                smask[:].unsqueeze(2).broadcast_to([P, QB, H]), ALU.mult).then_inc(fscale_done, 1)
                dve.wait_ge(fscale_done, b + 1)
                wait(dve, back_mm, BACK * (b - 1))
                v.tensor_tensor(pip[par][:].rearrange("p q (h n) -> p (q h) n", n=N_IP), fexp[:],
                                per_head(fscale), ALU.mult).then_inc(pip_done, 1)

            def output(b, par, pair, q):
                if not is_batch(b):
                    return
                dve.wait_ge(back_mm, BACK * b + 4 + q)
                if q == 0:
                    dve.wait_ge(xn_in[par], 16 * (pair + 1))
                    wait(dve, stored[par], 16 * pair)
                v.tensor_tensor(y[par][:, q, :], sharedP[:, 0:C], xn[par][:, q, :], ALU.add).then_inc(back_free, 1)

            def batch(b, par, pair):
                for u in range(UNITS):
                    if u in (5, 6):
                        output(b - 2, par, pair - 1, u - 5)
                    if u >= 2:
                        y_times_p(b, par, u - 2)
                    else:
                        y_times_p(b - 1, 1 - par, u - 2 + UNITS)
                    if u + 1 < UNITS:
                        softmax_shift(b, par, u + 1)
                    else:
                        softmax_shift(b + 1, 1 - par, 0)
                    if u == 3:
                        z_columns(b + 1, 1 - par)
                        norms(b - 1, 1 - par)
                    if u == 8:
                        ip_scores(b - 1, 1 - par)
                    if u == 9:
                        ip_probs(b - 1, 1 - par)

            every_batch(dve, batch)

        @block.gpsimd
        def _(pool):
            g = nc.gpsimd
            g.memset(scale_c[:], SCALE)
            g.memset(expo[:], -0.5).then_inc(expo_set, 1)
            pool.wait_ge(expo_set, 1)
            pool.wait_ge(ip_floor, 1)
            g.tensor_tensor(ipinv[:], ipinv[:], expo[:].broadcast_to([P, B * N_IP]), ALU.pow).then_inc(ip_inv, 1)
            pool.wait_ge(consts_in, N_CONSTS)
            pool.wait_ge(kip_ready, 1)

            def ip_columns(b, par, u):
                if not is_unit(b, u):
                    return
                pool.wait_ge(shift_done, UNITS * b + u + 1)
                if u == 0:
                    wait(pool, fused_done, b - 1)
                g.tensor_tensor(sip[par][:, slot(u), :], shifted[:, u % 2, :, T:T_ALL],
                                scale_c[:].unsqueeze(2).broadcast_to([P, HU, N_IP]), ALU.mult).then_inc(sip_done, 1)

            def halve(b, par, u):
                if not is_unit(b, u):
                    return
                pool.wait_ge(yp_done, UNITS * b + u + 1)
                wait(pool, yq_done, UNITS * b + u)
                g.tensor_tensor(half1[:], yp[:, u % 2, :, 0:T // 2], yp[:, u % 2, :, T // 2:T],
                                ALU.add).then_inc(half1_done, 1)
                pool.wait_ge(half1_done, UNITS * b + u + 1)
                if u == 0:
                    wait(pool, norm2_done, b - 1)
                g.tensor_tensor(yq[par][:, slot(u), :], half1[:, :, 0:TH], half1[:, :, TH:2 * TH],
                                ALU.add).then_inc(yq_done, 1)

            def k_blocks(b, par, m):
                if not is_batch(b):
                    return
                rows, heads = ROWS[m], ROWS[m] // DH
                if m == 0:
                    pool.wait_ge(front_free, FRONT * b + 3)
                    wait(pool, scores_mm, UNITS * (b - 1))
                to = kbd[par][0:rows, m * (P // DH):m * (P // DH) + heads, :]

                def spread(cols, k):
                    w = cols.stop - cols.start
                    return g.tensor_tensor(
                        to[:, :, cols], k.unsqueeze(1).broadcast_to([rows, heads, w]),
                        headmask[0:rows, 0:heads].unsqueeze(2).broadcast_to([rows, heads, w]), ALU.mult)

                spread(slice(0, T), kT[par][0:rows, m, :])
                last = spread(slice(T, T_ALL), kipT[0:rows, m, bass.ds(b * N_IP, N_IP)])
                if m == KC - 1:
                    last.then_inc(kbd_ready, 1)

            def vip_blocks(b, par, pair):
                if not is_batch(b):
                    return
                pool.wait_ge(vip_in[par], 16 * (pair + 1))
                wait(pool, back_mm, BACK * (b - 1))
                g.tensor_tensor(vbd[par][:], viprep[par][:], ipmask[:], ALU.mult).then_inc(vbd_ready, 1)

            def batch(b, par, pair):
                for u in range(UNITS):
                    if u + 1 < UNITS:
                        ip_columns(b, par, u + 1)
                    else:
                        ip_columns(b + 1, 1 - par, 0)
                    if u >= 2:
                        halve(b, par, u - 2)
                    else:
                        halve(b - 1, 1 - par, u - 2 + UNITS)
                    if u in (3, 4):
                        for m in ((0,), (1, 2))[u - 3]:
                            k_blocks(b + 1, 1 - par, m)
                    if u == 5 and is_batch(b - 1):
                        pool.wait_ge(norm2c_done, b)
                        wait(pool, cos_done, b - 1)
                        g.tensor_tensor(rnorm[:], norm2c[:], expo[:].broadcast_to([P, QB * H]),
                                        ALU.pow).then_inc(rnorm_done, 1)
                    if u == 8:
                        vip_blocks(b - 1, 1 - par, pair - 1 + par)

            every_batch(pool, batch)


def kernel(**inputs):
    import numpy as np
    import concourse.bacc as bacc
    from concourse.bass_utils import run_bass_kernel_spmd

    f = {k: np.asarray(a) for k, a in inputs.items()}
    x, c = f["x"], f["ctx_2048"]
    xt = x.transpose(0, 2, 1)
    ct = c.transpose(0, 2, 1).reshape(B, KE, P, T_ALL)
    ip = c[:, T:, :].reshape(B * N_IP, KE, P)
    heads_of_rows = np.arange(P) // DH
    arrays = {
        "x": x,
        "xt01": xt[:, :2 * P].reshape(B, 2, P, S).transpose(0, 2, 1, 3),
        "xt2": xt[:, 2 * P:],
        "ctxt": ct.transpose(0, 2, 1, 3),
        "ipt": ip.transpose(2, 1, 0),
        "mask": f["fside_S_0"].reshape(QB, P).T,
        "wq": f["L0_xattn_W_q"], "wk": f["L0_xattn_W_k"], "wv": f["L0_xattn_W_v"],
        "wki": f["L0_xattn_W_k_ip"], "wvi": f["L0_xattn_W_v_ip"], "wo": f["L0_xattn_W_out"],
        "bo": f["L0_xattn_b_out"].reshape(1, C),
        "ident": np.eye(P, dtype=np.float32),
        "headmask": (heads_of_rows[:, None] == np.arange(P // DH)[None]).astype(np.float32),
        "ipmask": (np.arange(H * N_IP)[:, None] // N_IP == np.arange(C)[None] // DH).astype(np.float32),
    }
    nc = bacc.Bacc("TRN2", target_bir_lowering=False, num_devices=1)
    ins, args = {}, []
    for name, a in arrays.items():
        a = np.ascontiguousarray(a)
        ins[f"in_{name}"] = a
        args.append(nc.dram_tensor(f"in_{name}", a.shape, mybir.dt.from_np(a.dtype), kind="ExternalInput").ap())
    args.append(nc.dram_tensor("out_y", (B, S, C), mybir.dt.float32, kind="ExternalOutput").ap())
    cross_attention(nc, *args)
    r = run_bass_kernel_spmd(nc, [ins], core_ids=[0])
    return r.results[0]["out_y"]
```

```python
import concourse.bass as bass
from concourse import mybir
from contextlib import ExitStack

B, S, C = 32, 256, 320
T_ALL, E = 120, 512
N_IP = 4
T = T_ALL - N_IP
H = 20
DH = C // H
SCALE = DH ** -0.5
SEM_SCALE = 0.5
EPS = 1e-12
P = 128
QB = S // P
KC, KE = 3, E // P
ROWS = [P, P, C - 2 * P]
PAIRS = H // 2
QUAD = 2 * DH
HU = 4
UNITS = H // HU * QB
ALL = B * UNITS
ZW = N_IP + 2 + DH
BLK = ZW + T + ZW
YW = ZW + T
TH = T // 4
KQ = 3
VG = 2
POWS = 5
BACK = 5


def cross_attention(nc, x, xt01, xt2, ctxt, ipt, mask, wq, wk, wv, wki, wvi, wo, bo,
                    ident_c, headmask_c, ipmask_c, out):
    f32, f32r = mybir.dt.float32, mybir.dt.float32r
    ALU = mybir.AluOpType
    ACT = mybir.ActivationFunctionType
    AX = mybir.AxisListType.X

    ctx = ExitStack()
    with ctx:
        def sb(name, shape, dt=f32):
            return ctx.enter_context(nc.sbuf_tensor(name, shape, dt))

        def ps(name, shape):
            return ctx.enter_context(nc.psum_tensor(name, shape, f32))

        def sem(name):
            return ctx.enter_context(nc.semaphore(name))

        Wq, Wo = sb("Wq", [P, KC, C]), sb("Wo", [P, KC, C])
        Wk, Wv = sb("Wk", [P, KE, C]), sb("Wv", [P, KE, C])
        Wki, Wvi = sb("Wki", [P, KE, C]), sb("Wvi", [P, KE, C])
        ident, ones = sb("ident", [P, P]), sb("ones", [P, P])
        headmask = sb("headmask", [P, 2])
        ipmask = sb("ipmask", [H * N_IP, C])
        smask = sb("smask", [P, QB])
        expo = sb("expo", [P, 1])
        scale_c = sb("scale_c", [P, 1])
        ipT, ipT2 = sb("ipT", [P, KE, B * N_IP]), sb("ipT2", [P, KE, B * N_IP])
        ipinv = sb("ipinv", [P, B * N_IP])
        kipT = sb("kipT", [P, KC, B * N_IP])
        kiphi = sb("kiphi", [P, KC, B * N_IP], f32r)
        kiplo = sb("kiplo", [P, KC, B * N_IP], f32r)
        kdiphi = sb("kdiphi", [P, KC, 2, B * N_IP], f32r)
        kdiplo = sb("kdiplo", [P, KC, 2, B * N_IP], f32r)
        vip = sb("vip", [B * N_IP, C])
        xT = [sb(f"xT{i}", [P, KC, S]) for i in range(2)]
        cT = [sb(f"cT{i}", [P, KE, T_ALL]) for i in range(2)]
        xn = [sb(f"xn{i}", [P, QB, C]) for i in range(2)]
        viprep = [sb(f"viprep{i}", [H * N_IP, C]) for i in range(2)]
        qhi, qlo = sb("qhi", [P, KC, S], f32r), sb("qlo", [P, KC, S], f32r)
        khi, klo = sb("khi", [P, KC, T], f32r), sb("klo", [P, KC, T], f32r)
        kdhi, kdlo = sb("kdhi", [P, KC, 2, T_ALL], f32r), sb("kdlo", [P, KC, 2, T_ALL], f32r)
        qs = [sb(f"qs{i}", [P, PAIRS, S], f32r) for i in range(2)]
        ks = [sb(f"ks{i}", [P, PAIRS, 2 * T_ALL], f32r) for i in range(2)]
        rhs = [sb(f"rhs{i}", [T, H // 2, BLK]) for i in range(2)]
        vbd = [sb(f"vbd{i}", [H * N_IP, C]) for i in range(2)]
        rowmax = sb("rowmax", [P, 2, HU])
        shifted = sb("shifted", [P, 4, HU, T_ALL])
        prob = sb("prob", [P, 4, HU, T])
        probT = sb("probT", [T, 2, HU, P])
        yp = sb("yp", [P, 4, HU, T])
        half1 = sb("half1", [P, HU, T // 2])
        yq = [sb(f"yq{i}", [P, QB * H, TH]) for i in range(2)]
        zlo = [sb(f"zlo{i}", [P, QB * H, ZW]) for i in range(2)]
        sip = [sb(f"sip{i}", [P, QB * H, N_IP]) for i in range(2)]
        norm2, floor2, norm2c, rnorm, rl = (sb(n, [P, QB * H]) for n in
                                            ("norm2", "floor2", "norm2c", "rnorm", "rl"))
        cosn = sb("cosn", [P, QB * H, N_IP])
        fused = sb("fused", [P, QB * H, N_IP])
        fmax, fsum, frec, fscale = (sb(n, [P, QB * H]) for n in ("fmax", "fsum", "frec", "fscale"))
        fsh = sb("fsh", [P, QB * H, N_IP])
        fexp = sb("fexp", [P, QB * H, N_IP])
        pip = [sb(f"pip{i}", [P, QB, H * N_IP]) for i in range(2)]
        on = [sb(f"on{i}", [P, QB, C]) for i in range(2)]
        pipT = sb("pipT", [H * N_IP, S])
        oT = sb("oT", [P, KC, S])
        y = [sb(f"y{i}", [P, QB, C]) for i in range(2)]

        scoresP = [ps(f"scoresP{i}", [P, 512]) for i in range(2)]
        transP = ps("transP", [P, 512])
        sharedP = ps("sharedP", [P, 512])
        yP = [ps(f"yP{i}", [P, 2, 512]) for i in range(2)]

        vip_dram = nc.dram_tensor("vip_scratch", (B, N_IP, C), f32, kind="Internal").ap()

        weights_in, consts_in, vip_out = sem("weights_in"), sem("consts_in"), sem("vip_out")
        batch_in = [sem(f"batch_in{i}") for i in range(2)]
        xn_in = [sem(f"xn_in{i}") for i in range(2)]
        vip_in = [sem(f"vip_in{i}") for i in range(2)]
        qs_in = [sem(f"qs_in{i}") for i in range(2)]
        ks_in = [sem(f"ks_in{i}") for i in range(2)]
        stored = [sem(f"stored{i}") for i in range(2)]
        preset, expo_set, ip_squared = sem("preset"), sem("expo_set"), sem("ip_squared")
        ip_norm_mm, ip_k_mm, ip_v_mm = sem("ip_norm_mm"), sem("ip_k_mm"), sem("ip_v_mm")
        kip_split, kdip_ready = sem("kip_split"), sem("kdip_ready")
        ip_floor, ip_inv, kip_ready, vip_ready = (sem("ip_floor"), sem("ip_inv"), sem("kip_ready"),
                                                  sem("vip_ready"))
        scores_mm, max_done, shift_done, exp_done = (sem("scores_mm"), sem("max_done"),
                                                     sem("shift_done"), sem("exp_done"))
        trans_mm, probT_ready, y_mm, yp_done, zlo_done = (sem("trans_mm"), sem("probT_ready"),
                                                          sem("y_mm"), sem("yp_done"), sem("zlo_done"))
        sip_done, half1_done, yq_done = sem("sip_done"), sem("half1_done"), sem("yq_done")
        kq_mm, kq_free = sem("kq_mm"), sem("kq_free")
        vg_mm, vg_free = sem("vg_mm"), sem("vg_free")
        back_mm, back_free = sem("back_mm"), sem("back_free")
        g_copied, hi_done, kd_ready, vbd_ready = (sem("g_copied"), sem("hi_done"), sem("kd_ready"),
                                                  sem("vbd_ready"))
        norm2_done, floor_done, rl_done, norm2c_done, rnorm_done, on_done = (
            sem("norm2_done"), sem("floor_done"), sem("rl_done"), sem("norm2c_done"),
            sem("rnorm_done"), sem("on_done"))
        cos_done, fused_done, fmax_done, fsh_done, fexp_done = (
            sem("cos_done"), sem("fused_done"), sem("fmax_done"), sem("fsh_done"), sem("fexp_done"))
        fsum_done, frec_done, fscale_done, pip_done = (sem("fsum_done"), sem("frec_done"),
                                                       sem("fscale_done"), sem("pip_done"))

        block = ctx.enter_context(nc.Block())

        N_WEIGHTS = 16 * 10
        N_CONSTS = 16 * 4

        def wait(eng, s, n):
            if not isinstance(n, int) or n > 0:
                eng.wait_ge(s, n)

        def is_unit(b, u):
            return not isinstance(b, int) or 0 <= UNITS * b + u < ALL

        def is_batch(b):
            return not isinstance(b, int) or 0 <= b < B

        def every_batch(eng, batch):
            for b in (-2, -1, 0, 1):
                batch(b, b % 2, b // 2)
            with eng.Fori(1, B // 2 - 2) as i:
                for par in range(2):
                    batch(i * 2 + par, par, i)
            for b in range(B - 4, B + 2):
                batch(b, b % 2, b // 2)

        def parts_in(s, pair):
            return s, 256 * (pair + 1)

        def slot(u):
            u %= UNITS
            return slice(u % QB * H + u // QB * HU, u % QB * H + u // QB * HU + HU)

        @block.sync
        def _(sp):
            sp.dma_start(ipT[:], ipt).then_inc(weights_in, 16)
            sp.dma_start(Wki[:], wki.rearrange("(k p) n -> p k n", p=P)).then_inc(weights_in, 16)
            sp.dma_start(Wvi[:], wvi.rearrange("(k p) n -> p k n", p=P)).then_inc(weights_in, 16)
            for w, src in ((Wq, wq), (Wo, wo)):
                sp.dma_start(w[:, 0:2, :], src[0:2 * P, :].rearrange("(k p) n -> p k n", p=P)).then_inc(
                    weights_in, 16)
                sp.dma_start(w[0:ROWS[2], 2, :], src[2 * P:C, :]).then_inc(weights_in, 16)
            sp.dma_start(Wo[ROWS[2]:ROWS[2] + 1, 2, :], bo).then_inc(weights_in, 16)
            sp.dma_start(Wk[:], wk.rearrange("(k p) n -> p k n", p=P)).then_inc(weights_in, 16)
            sp.dma_start(Wv[:], wv.rearrange("(k p) n -> p k n", p=P)).then_inc(weights_in, 16)

            def load_batch(b, par):
                sp.dma_start(xT[par][:, 0:2, :], xt01[b]).then_inc(batch_in[par], 16)
                sp.dma_start(xT[par][0:ROWS[2], 2, :], xt2[b]).then_inc(batch_in[par], 16)
                sp.dma_start(cT[par][:], ctxt[b]).then_inc(batch_in[par], 16)

            def copy_parts(stack, hi, lo, parts, s):
                for r in range(P // QUAD):
                    n = len(range(r, PAIRS, P // QUAD))
                    for i, part in enumerate(parts):
                        src = (hi, lo)[part][QUAD * r:QUAD * (r + 1), 0:n]
                        if len(src.shape) == 4:
                            src = src.rearrange("p m e t -> p m (e t)")
                        sp.dma_start(stack[QUAD * i:QUAD * (i + 1), r:PAIRS:P // QUAD, :].bitcast(f32),
                                     src.bitcast(f32)).then_inc(s, 16)

            load_batch(0, 0)

            def batch(b, par, pair):
                if is_batch(b + 3):
                    wait(sp, vg_mm, VG * (b + 2))
                    load_batch(b + 3, 1 - par)
                if isinstance(b, int) and b == -1:
                    sp.wait_ge(vip_ready, 1)
                    sp.dma_start(vip_dram.rearrange("b n c -> (b n) c"), vip[:]).then_inc(vip_out, 16)
                    sp.wait_ge(vip_out, 16)
                if is_batch(b):
                    wait(sp, vbd_ready, b - 1)
                    sp.dma_start(viprep[par][:], vip_dram[b].unsqueeze(0).broadcast_to(
                        [H, N_IP, C])).then_inc(vip_in[par], 16)
                    wait(sp, back_free, BACK * (b - 1))
                    sp.dma_start(xn[par][:], x[b].rearrange("(q p) c -> p q c", p=P)).then_inc(
                        xn_in[par], 16)
                if is_batch(b - 2):
                    wait(sp, back_free, BACK * (b - 1))
                    sp.dma_start(out[b - 2].rearrange("(q p) c -> p q c", p=P), y[par][:]).then_inc(
                        stored[par], 16)
                if is_batch(b + 2):
                    sp.wait_ge(kd_ready, b + 3)
                    copy_parts(ks[par], kdhi, kdlo, (0, 1, 0, 1), ks_in[par])
                    sp.wait_ge(kq_free, KQ * (b + 3))
                    copy_parts(qs[par], qhi, qlo, (0, 0, 1, 1), qs_in[par])

            every_batch(sp, batch)
            for par in range(2):
                sp.wait_ge(stored[par], 16 * (B // 2))

        @block.tensor
        def _(pe):
            mm, tr = nc.tensor.matmul, nc.tensor.transpose

            pe.wait_ge(preset, 1)
            pe.wait_ge(ip_squared, 1)
            for k in range(KE):
                last = mm(transP[:, 0:B * N_IP], ones[:], ipT2[:, k, :], start=k == 0, stop=k == KE - 1)
            last.then_inc(ip_norm_mm, 1)
            pe.wait_ge(weights_in, N_WEIGHTS)
            for m in range(KC):
                for k in range(KE):
                    last = mm(sharedP[0:ROWS[m], m * P:(m + 1) * P], Wki[:, k, m * P:m * P + ROWS[m]],
                              ipT[:, k, :], start=k == 0, stop=k == KE - 1)
            last.then_inc(ip_k_mm, 1)
            for k in range(KE):
                last = mm(scoresP[0][:, 0:C], ipT[:, k, :], Wvi[:, k, :], start=k == 0, stop=k == KE - 1)
            last.then_inc(ip_v_mm, 1)
            pe.wait_ge(consts_in, N_CONSTS)
            pe.wait_ge(kip_ready, 1)
            pe.wait_ge(vip_ready, 1)
            pe.wait_ge(ip_floor, 1)

            def kq(b, par, pair, piece):
                if not is_batch(b):
                    return
                if piece == 0:
                    pe.wait_ge(batch_in[par], 48 * (pair + 1))
                    wait(pe, back_free, BACK * (b - 3))
                    if isinstance(b, int) and 0 < b < 4:
                        pe.wait_ge(vg_free, VG * b)
                wait(pe, kq_free, KQ * b + piece)
                if piece == 0:
                    for m in range(KC):
                        for k in range(KE):
                            last = mm(sharedP[0:ROWS[m], m * T:(m + 1) * T],
                                      Wk[:, k, m * P:m * P + ROWS[m]], cT[par][:, k, 0:T],
                                      start=k == 0, stop=k == KE - 1)
                elif piece == 1:
                    for m in range(2):
                        for k in range(KC):
                            last = mm(sharedP[:, m * S:(m + 1) * S], Wq[0:ROWS[k], k, m * P:(m + 1) * P],
                                      xT[par][0:ROWS[k], k, :], start=k == 0, stop=k == KC - 1)
                else:
                    for k in range(KC):
                        last = mm(sharedP[0:ROWS[2], 0:S], Wq[0:ROWS[k], k, 2 * P:C],
                                  xT[par][0:ROWS[k], k, :], start=k == 0, stop=k == KC - 1)
                last.then_inc(kq_mm, 1)

            def vg(b, par, pair, piece):
                if not is_batch(b):
                    return
                if piece == 0:
                    pe.wait_ge(kq_free, KQ * (b + 1))
                wait(pe, vg_free, VG * b + piece)
                if piece == 0:
                    for k in range(KE):
                        last = mm(sharedP[0:T, 0:C], cT[par][:, k, 0:T], Wv[:, k, :],
                                  start=k == 0, stop=k == KE - 1)
                else:
                    for k in range(KE):
                        last = mm(sharedP[0:T, 0:T_ALL], cT[par][:, k, 0:T], cT[par][:, k, :],
                                  start=k == 0, stop=k == KE - 1)
                last.then_inc(vg_mm, 1)

            def back(b, par, pair, piece):
                if not is_batch(b):
                    return
                if piece == 0:
                    n = VG * (b + 4)
                    pe.wait_ge(vg_free, min(n, VG * B) if isinstance(n, int) else n)
                if piece == 0:
                    pe.wait_ge(pip_done, b + 1)
                wait(pe, back_free, BACK * b + piece)
                if piece == 0:
                    for q in range(QB):
                        last = tr(sharedP[0:H * N_IP, q * P:(q + 1) * P], pip[par][:, q, :], ident[:])
                elif piece in (1, 2):
                    if piece == 1:
                        pe.wait_ge(on_done, b + 1)
                        pe.wait_ge(vbd_ready, b + 1)
                    tiles = (0, 1) if piece == 1 else (2,)
                    for m in tiles:
                        mm(sharedP[0:ROWS[m], m % 2 * S:m % 2 * S + S], vbd[par][:, m * P:m * P + ROWS[m]],
                           pipT[:], start=m == tiles[0], stop=False, skip_group_check=True)
                    for m in tiles:
                        for q in range(QB):
                            at = m % 2 * S + q * P
                            last = mm(sharedP[0:ROWS[m], at:at + P], on[par][:, q, m * P:m * P + ROWS[m]],
                                      ident[:], start=False, stop=True, is_transpose=True,
                                      skip_group_check=True)
                else:
                    q = piece - 3
                    for m in range(KC):
                        rows = ROWS[m] + (m == KC - 1)
                        last = mm(sharedP[:, 0:C], oT[0:rows, m, q * P:(q + 1) * P], Wo[0:rows, m, :],
                                  start=m == 0, stop=m == KC - 1)
                last.then_inc(back_mm, 1)

            def scores(b, par, pair, u):
                if not is_unit(b, u):
                    return
                g, q = u // QB, u % QB
                if u == 0:
                    pe.wait_ge(*parts_in(qs_in[par], pair))
                    pe.wait_ge(*parts_in(ks_in[par], pair))
                wait(pe, shift_done, UNITS * b + u - 1)
                for j in range(2):
                    last = mm(scoresP[u % 2][:, 2 * T_ALL * j:2 * T_ALL * (j + 1)],
                              qs[par][:, 2 * g + j, q * P:(q + 1) * P], ks[par][:, 2 * g + j, :],
                              start=True, stop=True)
                last.then_inc(scores_mm, 1)

            def transposes(b, par, u):
                if not is_unit(b, u):
                    return
                pe.wait_ge(exp_done, UNITS * b + u + 1)
                wait(pe, probT_ready, UNITS * b + u)
                for h in range(HU):
                    last = tr(transP[0:T, h * P:(h + 1) * P], prob[:, (2 * par + u) % 4, h, :], ident[:])
                last.then_inc(trans_mm, 1)

            def products(b, par, u):
                if not is_unit(b, u):
                    return
                if u == 0:
                    pe.wait_ge(vg_free, VG * (b + 1))
                pe.wait_ge(probT_ready, UNITS * b + u + 1)
                wait(pe, yp_done, UNITS * b + u - 1)
                wait(pe, zlo_done, UNITS * b + u - 1)
                for h in range(HU):
                    r = h % 2
                    last = mm(yP[u % 2][:, h // 2, r * YW:(r + 1) * YW], probT[:, u % 2, h, :],
                              rhs[par][:, u // QB * 2 + h // 2, r * ZW:r * ZW + YW], start=True, stop=True)
                last.then_inc(y_mm, 1)

            SHARED = [(vg, 1, 0), (vg, 1, 1), (back, -2, 0), (back, -2, 1), (back, -2, 2),
                      (back, -2, 3), (back, -2, 4), (kq, 2, 0), (kq, 2, 1), (kq, 2, 2)]

            def batch(b, par, pair):
                for u in range(UNITS):
                    what, off, piece = SHARED[u]
                    what(b + off, (par + off) % 2, pair + (par + off) // 2, piece)
                    if u + 2 < UNITS:
                        scores(b, par, pair, u + 2)
                    else:
                        scores(b + 1, 1 - par, pair + par, u + 2 - UNITS)
                    transposes(b, par, u)
                    if u:
                        products(b, par, u - 1)
                    else:
                        products(b - 1, 1 - par, UNITS - 1)

            every_batch(pe, batch)

        @block.scalar
        def _(act):
            copy = nc.scalar.copy
            act.dma_start(ident[:], ident_c).then_inc(consts_in, 16)
            act.dma_start(headmask[:], headmask_c).then_inc(consts_in, 16)
            act.dma_start(ipmask[:], ipmask_c).then_inc(consts_in, 16)
            act.dma_start(smask[:], mask).then_inc(consts_in, 16)

            act.wait_ge(ip_k_mm, 1)
            act.wait_ge(preset, 1)
            copy(kipT[:, 0:2, :], sharedP[:, 0:2 * P].rearrange("p (m n) -> p m n", m=2))
            copy(kipT[0:ROWS[2], 2, :], sharedP[0:ROWS[2], 2 * P:3 * P]).then_inc(kip_ready, 1)
            act.wait_ge(ip_v_mm, 1)
            copy(vip[:], scoresP[0][:, 0:C]).then_inc(vip_ready, 1)

            def kq(b, par, pair, piece):
                if not is_batch(b):
                    return
                act.wait_ge(kq_mm, KQ * b + piece + 1)
                if piece == 0:
                    wait(act, kd_ready, b)
                    copy(khi[:, 0:2, :], sharedP[:, 0:2 * T].rearrange("p (m t) -> p m t", m=2))
                    copy(khi[0:ROWS[2], 2, :], sharedP[0:ROWS[2], 2 * T:3 * T]).then_inc(hi_done, 1)
                elif piece == 1:
                    if not isinstance(b, int) or b > 0:
                        act.wait_ge(*parts_in(qs_in[1 - par], pair - 1 + par))
                    copy(qhi[:, 0:2, :], sharedP[:, 0:2 * S].rearrange("p (m s) -> p m s", m=2)
                         ).then_inc(hi_done, 1)
                else:
                    copy(qhi[0:ROWS[2], 2, :], sharedP[0:ROWS[2], 0:S]).then_inc(hi_done, 1)

            def vg(b, par, pair, piece):
                if not is_batch(b):
                    return
                act.wait_ge(vg_mm, VG * b + piece + 1)
                if piece == 0:
                    wait(act, y_mm, UNITS * (b - 1))
                    for r in range(2):
                        at = r * YW + ZW - DH
                        last = copy(rhs[par][:, :, at:at + DH],
                                    sharedP[0:T, 0:C].rearrange("p (j r d) -> p r j d", r=2, d=DH)[:, r])
                    last.then_inc(vg_free, 1)
                else:
                    copy(rhs[par][:, :, ZW:YW], sharedP[0:T, 0:T].unsqueeze(1).broadcast_to(
                        [T, H // 2, T])).then_inc(g_copied, 1)

            def back(b, par, pair, piece):
                if not is_batch(b):
                    return
                if piece < 3:
                    act.wait_ge(back_mm, BACK * b + piece + 1)
                if piece == 0:
                    copy(pipT[:], sharedP[0:H * N_IP, 0:S]).then_inc(back_free, 1)
                elif piece == 1:
                    copy(oT[:, 0:2, :], sharedP[:, 0:2 * S].rearrange("p (m s) -> p m s", m=2)
                         ).then_inc(back_free, 1)
                elif piece == 2:
                    copy(oT[0:ROWS[2], 2, :], sharedP[0:ROWS[2], 0:S]).then_inc(back_free, 1)

            def evac_trans(b, par, u):
                if not is_unit(b, u):
                    return
                act.wait_ge(trans_mm, UNITS * b + u + 1)
                wait(act, y_mm, UNITS * b + u - 1)
                copy(probT[:, u % 2, :, :], transP[0:T, :].rearrange("t (h s) -> t h s", h=HU)
                     ).then_inc(probT_ready, 1)

            def exp_unit(b, par, u):
                if not is_unit(b, u):
                    return
                act.wait_ge(shift_done, UNITS * b + u + 1)
                wait(act, yp_done, UNITS * b + u - 3)
                nc.scalar.activation(prob[:, (2 * par + u) % 4, :, :], shifted[:, (2 * par + u) % 4, :, 0:T], ACT.Exp,
                                     scale=SCALE).then_inc(exp_done, 1)

            def evac_zlo(b, par, u):
                if not is_unit(b, u):
                    return
                act.wait_ge(yp_done, UNITS * b + u + 1)
                if u == 0:
                    wait(act, cos_done, b - 1)
                    wait(act, on_done, b - 1)
                z = yP[u % 2][:, :, 0:2 * YW]
                for r in range(2):
                    at = r * (YW + T)
                    dst = zlo[par][:, slot(u), :].rearrange("p (k r) z -> p r k z", r=2)[:, r]
                    last = copy(dst, z[:, :, at:at + ZW])
                last.then_inc(zlo_done, 1)

            SHARED = [(vg, 1, 0), (vg, 1, 1), (back, -2, 0), (back, -2, 1), (back, -2, 2),
                      (back, -2, 3), (back, -2, 4), (kq, 2, 0), (kq, 2, 1), (kq, 2, 2)]

            def batch(b, par, pair):
                for u in range(UNITS):
                    what, off, piece = SHARED[u]
                    what(b + off, (par + off) % 2, pair + (par + off) // 2, piece)
                    evac_trans(b, par, u)
                    if u + 1 < UNITS:
                        exp_unit(b, par, u + 1)
                    else:
                        exp_unit(b + 1, 1 - par, 0)
                    if u >= 2:
                        evac_zlo(b, par, u - 2)
                    else:
                        evac_zlo(b - 1, 1 - par, u - 2 + UNITS)
                    if u == 8 and is_batch(b - 1):
                        act.wait_ge(fsh_done, b)
                        wait(act, pip_done, b - 1)
                        nc.scalar.activation(fexp[:], fsh[:], ACT.Exp).then_inc(fexp_done, 1)

            every_batch(act, batch)

        @block.vector
        def _(dve):
            v = nc.vector
            v.memset(ones[:], 1.0)
            for t in (khi, klo, kipT):
                v.memset(t[:].bitcast(f32), 0.0)
            for i in range(2):
                v.memset(rhs[i][:], 0.0)
            v.memset(oT[:], 1.0).then_inc(preset, 1)
            dve.wait_ge(preset, 1)
            for i in range(2):
                for r in range(2):
                    at = r * (YW + 0) + N_IP
                    v.memset(rhs[i][:, :, at:at + 1], 1.0)
            dve.wait_ge(weights_in, N_WEIGHTS)
            v.tensor_tensor(ipT2[:], ipT[:], ipT[:], ALU.mult).then_inc(ip_squared, 1)
            dve.wait_ge(kip_ready, 1)
            v.tensor_copy(kiphi[:], kipT[:]).then_inc(kip_split, 1)
            dve.wait_ge(kip_split, 1)
            v.tensor_tensor(kiplo[:], kipT[:], kiphi[:].bitcast(f32), ALU.subtract).then_inc(kip_split, 1)
            dve.wait_ge(ip_norm_mm, 1)
            v.tensor_scalar(ipinv[:], transP[:, 0:B * N_IP], EPS * EPS, 1.0 / SEM_SCALE ** 2,
                            ALU.max, ALU.mult).then_inc(ip_floor, 1)
            dve.wait_ge(consts_in, N_CONSTS)

            def softmax_shift(b, par, u):
                if not is_unit(b, u):
                    return
                sc = scoresP[u % 2][:, 0:HU * T_ALL].rearrange("p (h t) -> p h t", h=HU)
                dve.wait_ge(scores_mm, UNITS * b + u + 1)
                v.tensor_reduce(rowmax[:, u % 2, :], sc[:, :, 0:T], AX, ALU.max).then_inc(max_done, 1)
                dve.wait_ge(max_done, UNITS * b + u + 1)
                wait(dve, exp_done, UNITS * b + u - 3)
                wait(dve, sip_done, UNITS * b + u - 3)
                v.tensor_tensor(shifted[:, (2 * par + u) % 4, :, :], sc, rowmax[:, u % 2, :].unsqueeze(2).broadcast_to(
                    [P, HU, T_ALL]), ALU.subtract).then_inc(shift_done, 1)

            def y_times_p(b, par, u):
                if not is_unit(b, u):
                    return
                dve.wait_ge(y_mm, UNITS * b + u + 1)
                wait(dve, half1_done, UNITS * b + u - 3)
                yv = yP[u % 2][:, :, ZW:ZW + 2 * T].rearrange("p k (r t) -> p k r t", r=2)
                v.tensor_tensor(yp[:, (2 * par + u) % 4, :, :].rearrange("p (k r) t -> p k r t", r=2), yv,
                                prob[:, (2 * par + u) % 4, :, :].rearrange("p (k r) t -> p k r t", r=2),
                                ALU.mult).then_inc(yp_done, 1)

            def low_part(b, par, pair, piece):
                if not is_batch(b):
                    return
                dve.wait_ge(hi_done, 3 * b + piece + 1)
                if piece == 0:
                    wait(dve, kd_ready, b)
                    v.tensor_tensor(klo[:, 0:2, :], sharedP[:, 0:2 * T].rearrange("p (m t) -> p m t", m=2),
                                    khi[:, 0:2, :].bitcast(f32), ALU.subtract)
                    last = v.tensor_tensor(klo[0:ROWS[2], 2, :], sharedP[0:ROWS[2], 2 * T:3 * T],
                                           khi[0:ROWS[2], 2, :].bitcast(f32), ALU.subtract)
                elif piece == 1:
                    if not isinstance(b, int) or b > 0:
                        dve.wait_ge(*parts_in(qs_in[1 - par], pair - 1 + par))
                    last = v.tensor_tensor(qlo[:, 0:2, :], sharedP[:, 0:2 * S].rearrange("p (m s) -> p m s", m=2),
                                           qhi[:, 0:2, :].bitcast(f32), ALU.subtract)
                else:
                    last = v.tensor_tensor(qlo[0:ROWS[2], 2, :], sharedP[0:ROWS[2], 0:S],
                                           qhi[0:ROWS[2], 2, :].bitcast(f32), ALU.subtract)
                last.then_inc(kq_free, 1)

            def z_columns(b, par):
                if not is_batch(b):
                    return
                dve.wait_ge(g_copied, b + 1)
                if isinstance(b, int) and b == 0:
                    dve.wait_ge(ip_inv, 1)
                for r in range(2):
                    at = r * YW
                    last = v.tensor_tensor(
                        rhs[par][:, :, at:at + N_IP],
                        sharedP[0:T, T:T_ALL].unsqueeze(1).broadcast_to([T, H // 2, N_IP]),
                        ipinv[0:T, bass.ds(b * N_IP, N_IP)].unsqueeze(1).broadcast_to([T, H // 2, N_IP]),
                        ALU.mult)
                last.then_inc(vg_free, 1)

            def norms(b, par):
                if not is_batch(b):
                    return
                dve.wait_ge(yq_done, UNITS * (b + 1))
                dve.wait_ge(zlo_done, UNITS * (b + 1))
                z = zlo[par]
                v.tensor_reduce(norm2[:], yq[par][:], AX, ALU.add).then_inc(norm2_done, 1)
                v.scalar_tensor_tensor(floor2[:], z[:, :, N_IP], EPS * EPS, z[:, :, N_IP], ALU.mult,
                                       ALU.mult).then_inc(floor_done, 1)
                v.reciprocal(rl[:], z[:, :, N_IP]).then_inc(rl_done, 1)
                dve.wait_ge(norm2_done, b + 1)
                dve.wait_ge(floor_done, b + 1)
                wait(dve, rnorm_done, POWS * b)
                v.tensor_tensor(norm2c[:], norm2[:], floor2[:], ALU.max).then_inc(norm2c_done, 1)
                dve.wait_ge(rl_done, b + 1)
                wait(dve, back_mm, BACK * (b - 1))
                v.tensor_tensor(on[par][:].rearrange("p q (h d) -> p (q h) d", d=DH), z[:, :, ZW - DH:ZW],
                                rl[:].unsqueeze(2).broadcast_to([P, QB * H, DH]), ALU.mult).then_inc(on_done, 1)

            def per_head(t):
                return t[:].unsqueeze(2).broadcast_to([P, QB * H, N_IP])

            def ip_scores(b, par):
                if not is_batch(b):
                    return
                dve.wait_ge(rnorm_done, POWS * (b + 1))
                v.tensor_tensor(cosn[:], zlo[par][:, :, 0:N_IP], per_head(rnorm), ALU.mult).then_inc(cos_done, 1)
                dve.wait_ge(cos_done, b + 1)
                dve.wait_ge(sip_done, UNITS * (b + 1))
                v.tensor_tensor(fused[:], sip[par][:], cosn[:], ALU.add).then_inc(fused_done, 1)
                dve.wait_ge(fused_done, b + 1)
                v.tensor_reduce(fmax[:], fused[:], AX, ALU.max).then_inc(fmax_done, 1)
                dve.wait_ge(fmax_done, b + 1)
                wait(dve, fexp_done, b)
                v.tensor_tensor(fsh[:], fused[:], per_head(fmax), ALU.subtract).then_inc(fsh_done, 1)

            def ip_probs(b, par):
                if not is_batch(b):
                    return
                dve.wait_ge(fexp_done, b + 1)
                v.tensor_reduce(fsum[:], fexp[:], AX, ALU.add).then_inc(fsum_done, 1)
                dve.wait_ge(fsum_done, b + 1)
                v.reciprocal(frec[:], fsum[:]).then_inc(frec_done, 1)
                dve.wait_ge(frec_done, b + 1)
                v.tensor_tensor(fscale[:].rearrange("p (q h) -> p q h", q=QB),
                                frec[:].rearrange("p (q h) -> p q h", q=QB),
                                smask[:].unsqueeze(2).broadcast_to([P, QB, H]), ALU.mult).then_inc(fscale_done, 1)
                dve.wait_ge(fscale_done, b + 1)
                wait(dve, back_mm, BACK * (b - 1))
                v.tensor_tensor(pip[par][:].rearrange("p q (h n) -> p (q h) n", n=N_IP), fexp[:],
                                per_head(fscale), ALU.mult).then_inc(pip_done, 1)

            def output(b, par, pair, q):
                if not is_batch(b):
                    return
                dve.wait_ge(back_mm, BACK * b + 4 + q)
                if q == 0:
                    dve.wait_ge(xn_in[par], 16 * (pair + 1))
                    wait(dve, stored[par], 16 * pair)
                v.tensor_tensor(y[par][:, q, :], sharedP[:, 0:C], xn[par][:, q, :], ALU.add).then_inc(back_free, 1)

            def batch(b, par, pair):
                for u in range(UNITS):
                    if u >= 2:
                        y_times_p(b, par, u - 2)
                    else:
                        y_times_p(b - 1, 1 - par, u - 2 + UNITS)
                    if u + 1 < UNITS:
                        softmax_shift(b, par, u + 1)
                    else:
                        softmax_shift(b + 1, 1 - par, 0)
                    if u == 1:
                        z_columns(b + 1, 1 - par)
                    if u == 2:
                        norms(b - 1, 1 - par)
                    if u in (5, 6):
                        output(b - 2, par, pair - 1, u - 5)
                    if u in (7, 8, 9):
                        low_part(b + 2, par, pair + 1, u - 7)
                    if u == 8:
                        ip_scores(b - 1, 1 - par)
                    if u == 9:
                        ip_probs(b - 1, 1 - par)

            every_batch(dve, batch)

        @block.gpsimd
        def _(pool):
            g = nc.gpsimd
            def spread(dst, k, n):
                return g.tensor_tensor(dst, k.unsqueeze(2).broadcast_to([P, KC, 2, n]),
                                       headmask[:].unsqueeze(1).unsqueeze(3).broadcast_to([P, KC, 2, n]),
                                       ALU.mult)

            g.memset(scale_c[:], SCALE)
            g.memset(expo[:], -0.5).then_inc(expo_set, 1)
            pool.wait_ge(expo_set, 1)
            pool.wait_ge(ip_floor, 1)
            g.tensor_tensor(ipinv[:], ipinv[:], expo[:].broadcast_to([P, B * N_IP]), ALU.pow).then_inc(ip_inv, 1)
            pool.wait_ge(consts_in, N_CONSTS)
            pool.wait_ge(kip_split, 2)
            spread(kdiphi[:], kiphi[:].bitcast(f32), B * N_IP)
            spread(kdiplo[:], kiplo[:].bitcast(f32), B * N_IP).then_inc(kdip_ready, 1)
            pool.wait_ge(kdip_ready, 1)

            def ip_columns(b, par, u):
                if not is_unit(b, u):
                    return
                pool.wait_ge(shift_done, UNITS * b + u + 1)
                if u == 0:
                    wait(pool, fused_done, b - 1)
                g.tensor_tensor(sip[par][:, slot(u), :], shifted[:, (2 * par + u) % 4, :, T:T_ALL],
                                scale_c[:].unsqueeze(2).broadcast_to([P, HU, N_IP]), ALU.mult).then_inc(sip_done, 1)

            def halve(b, par, u):
                if not is_unit(b, u):
                    return
                pool.wait_ge(yp_done, UNITS * b + u + 1)
                wait(pool, yq_done, UNITS * b + u)
                buf = yp[:, (2 * par + u) % 4, :, :]
                g.tensor_tensor(half1[:], buf[:, :, 0:T // 2], buf[:, :, T // 2:T],
                                ALU.add).then_inc(half1_done, 1)
                pool.wait_ge(half1_done, UNITS * b + u + 1)
                if u == 0:
                    wait(pool, norm2_done, b - 1)
                g.tensor_tensor(yq[par][:, slot(u), :], half1[:, :, 0:TH], half1[:, :, TH:2 * TH],
                                ALU.add).then_inc(yq_done, 1)

            def k_blocks(b, par, pair):
                if not is_batch(b):
                    return
                pool.wait_ge(kq_free, KQ * b + 1)
                if not isinstance(b, int) or b > 0:
                    pool.wait_ge(*parts_in(ks_in[1 - par], pair - 1 + par))
                spread(kdhi[:, :, :, 0:T], khi[:].bitcast(f32), T)
                spread(kdlo[:, :, :, 0:T], klo[:].bitcast(f32), T)
                cols = bass.ds(b * N_IP, N_IP)
                for m in range(KC):
                    g.tensor_copy(kdhi[:, m, :, T:T_ALL], kdiphi[:, m, :, cols].bitcast(f32))
                    last = g.tensor_copy(kdlo[:, m, :, T:T_ALL], kdiplo[:, m, :, cols].bitcast(f32))
                last.then_inc(kd_ready, 1)

            def vip_blocks(b, par, pair):
                if not is_batch(b):
                    return
                pool.wait_ge(vip_in[par], 16 * (pair + 1))
                wait(pool, back_mm, BACK * (b - 1))
                g.tensor_tensor(vbd[par][:], viprep[par][:], ipmask[:], ALU.mult).then_inc(vbd_ready, 1)

            def batch(b, par, pair):
                for u in range(UNITS):
                    if u + 1 < UNITS:
                        ip_columns(b, par, u + 1)
                    else:
                        ip_columns(b + 1, 1 - par, 0)
                    if u >= 2:
                        halve(b, par, u - 2)
                    else:
                        halve(b - 1, 1 - par, u - 2 + UNITS)
                    if u == 8:
                        k_blocks(b + 2, par, pair + 1)
                    if 3 <= u < 3 + POWS and is_batch(b - 1):
                        if u == 3:
                            pool.wait_ge(norm2c_done, b)
                            wait(pool, cos_done, b - 1)
                        w = QB * H // POWS
                        cols = slice(w * (u - 3), w * (u - 2))
                        g.tensor_tensor(rnorm[:, cols], norm2c[:, cols], expo[:].broadcast_to([P, w]),
                                        ALU.pow).then_inc(rnorm_done, 1)
                    if u == 0:
                        vip_blocks(b - 1, 1 - par, pair - 1 + par)

            every_batch(pool, batch)


def kernel(**inputs):
    import numpy as np
    import concourse.bacc as bacc
    from concourse.bass_utils import run_bass_kernel_spmd

    f = {k: np.asarray(a) for k, a in inputs.items()}
    x, c = f["x"], f["ctx_2048"]
    xt = x.transpose(0, 2, 1)
    ct = c.transpose(0, 2, 1).reshape(B, KE, P, T_ALL)
    ip = c[:, T:, :].reshape(B * N_IP, KE, P)
    heads_of_rows = np.arange(P) // DH
    arrays = {
        "x": x,
        "xt01": xt[:, :2 * P].reshape(B, 2, P, S).transpose(0, 2, 1, 3),
        "xt2": xt[:, 2 * P:],
        "ctxt": ct.transpose(0, 2, 1, 3),
        "ipt": ip.transpose(2, 1, 0),
        "mask": f["fside_S_0"].reshape(QB, P).T,
        "wq": f["L0_xattn_W_q"], "wk": f["L0_xattn_W_k"], "wv": f["L0_xattn_W_v"],
        "wki": f["L0_xattn_W_k_ip"], "wvi": f["L0_xattn_W_v_ip"], "wo": f["L0_xattn_W_out"],
        "bo": f["L0_xattn_b_out"].reshape(1, C),
        "ident": np.eye(P, dtype=np.float32),
        "headmask": (heads_of_rows[:, None] % 2 == np.arange(2)[None]).astype(np.float32),
        "ipmask": (np.arange(H * N_IP)[:, None] // N_IP == np.arange(C)[None] // DH).astype(np.float32),
    }
    nc = bacc.Bacc("TRN2", target_bir_lowering=False, num_devices=1)
    ins, args = {}, []
    for name, a in arrays.items():
        a = np.ascontiguousarray(a)
        ins[f"in_{name}"] = a
        args.append(nc.dram_tensor(f"in_{name}", a.shape, mybir.dt.from_np(a.dtype), kind="ExternalInput").ap())
    args.append(nc.dram_tensor("out_y", (B, S, C), mybir.dt.float32, kind="ExternalOutput").ap())
    cross_attention(nc, *args)
    r = run_bass_kernel_spmd(nc, [ins], core_ids=[0])
    return r.results[0]["out_y"]
```

```python
import concourse.bass as bass
from concourse import mybir
from contextlib import ExitStack

B, S, C = 32, 256, 320
T_ALL, E = 120, 512
N_IP = 4
T = T_ALL - N_IP
H = 20
DH = C // H
SCALE = DH ** -0.5
SEM_SCALE = 0.5
EPS = 1e-12
P = 128
QB = S // P
KC, KE = 3, E // P
ROWS = [P, P, C - 2 * P]
PAIRS = H // 2
QUAD = 2 * DH
HU = 4
UNITS = H // HU * QB
ALL = B * UNITS
ZW = N_IP + 2 + DH
BLK = ZW + T + ZW
YW = ZW + T
CP = KC * P
KQ = 4
Q01, K_ROWS, K_TRANSPOSED, Q2 = range(KQ)
BACK = 5
PARTS = 3
COPIES = PARTS * P // QUAD
NORM_HEADS = ((0, 12), (12, H))
NORMS = len(NORM_HEADS)


def cross_attention(nc, x, xt01, xt2, ctxt, ipt, mask, wq, wk, wv, wki, wvi, wo, bo,
                    ident_c, headmask_c, ipmask_c, out):
    f32, f32r = mybir.dt.float32, mybir.dt.float32r
    ALU = mybir.AluOpType
    ACT = mybir.ActivationFunctionType
    AX = mybir.AxisListType.X

    ctx = ExitStack()
    with ctx:
        def sb(name, shape, dt=f32):
            return ctx.enter_context(nc.sbuf_tensor(name, shape, dt))

        def ps(name, shape):
            return ctx.enter_context(nc.psum_tensor(name, shape, f32))

        def sem(name):
            return ctx.enter_context(nc.semaphore(name))

        Wq = sb("Wq", [P, KC, CP])
        Wqhi, Wqlo = sb("Wqhi", [P, KC, CP], f32r), sb("Wqlo", [P, KC, CP], f32r)
        Wohi, Wolo = sb("Wohi", [P, KC, C], f32r), sb("Wolo", [P, KC, C], f32r)
        Wkhi, Wklo = sb("Wkhi", [P, KE, C], f32r), sb("Wklo", [P, KE, C], f32r)
        vchi, vclo = sb("vchi", [P, KE, C + P], f32r), sb("vclo", [P, KE, C + P], f32r)
        chi, clo = vchi[:, :, C:C + P], vclo[:, :, C:C + P]
        ident, ones = sb("ident", [P, P]), sb("ones", [P, P])
        headmask = sb("headmask", [P, 2])
        ipmask = sb("ipmask", [H * N_IP, C])
        smask = sb("smask", [P, QB])
        expo = sb("expo", [P, 1])
        ipinv = sb("ipinv", [P, B * N_IP])
        ipnorm = sb("ipnorm", [P, 1])
        kipT = sb("kipT", [P, KC, B * N_IP])
        kiphi = sb("kiphi", [P, KC, B * N_IP], f32r)
        kiplo = sb("kiplo", [P, KC, B * N_IP], f32r)
        kdiphi = sb("kdiphi", [P, KC, 2, B * N_IP], f32r)
        kdiplo = sb("kdiplo", [P, KC, 2, B * N_IP], f32r)
        vip = sb("vip", [B * N_IP, C])
        xT = [sb(f"xT{i}", [P, KC, S]) for i in range(2)]
        cT = [sb(f"cT{i}", [P, KE, T_ALL]) for i in range(2)]
        xn_both = sb("xn_both", [P, 2, QB, C])
        xn = [xn_both[:, i] for i in range(2)]
        viprep = [sb(f"viprep{i}", [H * N_IP, C]) for i in range(2)]
        xhi, xlo = sb("xhi", [P, KC, S], f32r), sb("xlo", [P, KC, S], f32r)
        qhi = [sb(f"qhi{i}", [P, KC, S], f32r) for i in range(2)]
        qlo = [sb(f"qlo{i}", [P, KC, S], f32r) for i in range(2)]
        khi, klo = sb("khi", [P, KC, T], f32r), sb("klo", [P, KC, T], f32r)
        k_rows = klo[0:T].rearrange("p m t -> p (m t)").bitcast(f32)[:, 0:C]
        ip_products = sb("ip_products", [T, N_IP])
        kdhi, kdlo = sb("kdhi", [P, KC, 2, T_ALL], f32r), sb("kdlo", [P, KC, 2, T_ALL], f32r)
        qs = [sb(f"qs{i}", [P, PAIRS, S], f32r) for i in range(2)]
        ks = [sb(f"ks{i}", [P, PAIRS, 2 * T_ALL], f32r) for i in range(2)]
        rhs = [sb(f"rhs{i}", [T, H // 2, BLK]) for i in range(2)]
        vbd = [sb(f"vbd{i}", [H * N_IP, C]) for i in range(2)]
        negmax = sb("negmax", [P, 2, HU])
        prob = sb("prob", [P, 4, HU, T])
        probT = sb("probT", [T, 2, HU, P])
        yp = sb("yp", [P, HU, T])
        norm2 = [sb(f"norm2{i}", [P, QB * H]) for i in range(2)]
        zlo = [sb(f"zlo{i}", [P, QB * H, ZW]) for i in range(2)]
        sip = [sb(f"sip{i}", [P, QB * H, N_IP]) for i in range(2)]
        floor2, norm2c, rnorm, rl = (sb(n, [P, QB * H]) for n in ("floor2", "norm2c", "rnorm", "rl"))
        cosn = sb("cosn", [P, QB * H, N_IP])
        fused = sb("fused", [P, QB * H, N_IP])
        fmax, fsum, frec, fscale = (sb(n, [P, QB * H]) for n in ("fmax", "fsum", "frec", "fscale"))
        fsh = sb("fsh", [P, QB * H, N_IP])
        fexp = sb("fexp", [P, QB * H, N_IP])
        pip = [sb(f"pip{i}", [P, QB, H * N_IP]) for i in range(2)]
        on_both = sb("on_both", [P, 2, QB, C])
        on = [on_both[:, i] for i in range(2)]
        pipT = sb("pipT", [H * N_IP, S])
        oThi, oTlo = sb("oThi", [P, KC, S], f32r), sb("oTlo", [P, KC, S], f32r)
        y_both = sb("y_both", [P, 2, QB, C])
        y = [y_both[:, i] for i in range(2)]

        def early(buffer, k, n):
            flat = buffer[:].rearrange("p a b -> p (a b)" if len(buffer.shape) == 3 else
                                       "p a b c -> p (a b c)")
            return flat[:, 0:k * n].rearrange("p (k n) -> p k n", k=k)

        Wk, Wv = early(prob, KE, C), sb("Wv", [P, KE, C])
        ipT, ipT2 = early(zlo[0], KE, B * N_IP), early(zlo[1], KE, B * N_IP)
        diag = early(sip[0], 1, P)
        Wki, Wvi, Wo = early(on_both, KE, C), early(y_both, KE, C), early(xn_both, KC, C)

        scoresP = [ps(f"scoresP{i}", [P, 512]) for i in range(2)]
        transP = ps("transP", [P, 512])
        sharedP = ps("sharedP", [P, 512])
        yP = [ps(f"yP{i}", [P, 2, 512]) for i in range(2)]

        vip_dram = nc.dram_tensor("vip_scratch", (B, N_IP, C), f32, kind="Internal").ap()

        wq_in, wk_in, ip_in, wvo_in = sem("wq_in"), sem("wk_in"), sem("ip_in"), sem("wvo_in")
        consts_in, vip_out = sem("consts_in"), sem("vip_out")
        batch_in = [sem(f"batch_in{i}") for i in range(2)]
        xn_in = [sem(f"xn_in{i}") for i in range(2)]
        vip_in = [sem(f"vip_in{i}") for i in range(2)]
        qs_in = [sem(f"qs_in{i}") for i in range(2)]
        ks_in = [sem(f"ks_in{i}") for i in range(2)]
        stored = [sem(f"stored{i}") for i in range(2)]
        w_high, w_split, stacks_cleared = sem("w_high"), sem("w_split"), sem("stacks_cleared")
        ip_power, ip_diag, ip_spread_mm = sem("ip_power"), sem("ip_diag"), sem("ip_spread_mm")
        preset, expo_set, ip_squared = sem("preset"), sem("expo_set"), sem("ip_squared")
        ip_norm_mm, ip_k_mm, ip_v_mm = sem("ip_norm_mm"), sem("ip_k_mm"), sem("ip_v_mm")
        kip_split, kdip_ready = sem("kip_split"), sem("kdip_ready")
        ip_floor, ip_inv, kip_ready, vip_ready = (sem("ip_floor"), sem("ip_inv"), sem("kip_ready"),
                                                  sem("vip_ready"))
        scores_mm, max_done, exp_done = sem("scores_mm"), sem("max_done"), sem("exp_done")
        trans_mm, probT_ready, y_mm, yp_done, zlo_done = (sem("trans_mm"), sem("probT_ready"),
                                                          sem("y_mm"), sem("yp_done"), sem("zlo_done"))
        kq_mm, kq_free = sem("kq_mm"), sem("kq_free")
        vg_mm, vg_free = sem("vg_mm"), sem("vg_free")
        back_mm, back_free = sem("back_mm"), sem("back_free")
        k_low, kd_ready, vbd_ready = sem("k_low"), sem("kd_ready"), sem("vbd_ready")
        q_low, g_spread = sem("q_low"), sem("g_spread")
        split_hi, x_split, context_split, oT_done = (sem("split_hi"), sem("x_split"),
                                                     sem("context_split"), sem("oT_done"))
        floor_done, rl_done, norm2c_done, rnorm_done, on_done = (
            sem("floor_done"), sem("rl_done"), sem("norm2c_done"),
            sem("rnorm_done"), sem("on_done"))
        cos_done, fused_done, fmax_done, fsh_done, fexp_done = (
            sem("cos_done"), sem("fused_done"), sem("fmax_done"), sem("fsh_done"), sem("fexp_done"))
        fsum_done, frec_done, fscale_done, pip_done = (sem("fsum_done"), sem("frec_done"),
                                                       sem("fscale_done"), sem("pip_done"))

        block = ctx.enter_context(nc.Block())

        N_CONSTS = 16 * 4

        def wait(eng, s, n):
            if not isinstance(n, int) or n > 0:
                eng.wait_ge(s, n)

        def is_unit(b, u):
            return not isinstance(b, int) or 0 <= UNITS * b + u < ALL

        def is_batch(b):
            return not isinstance(b, int) or 0 <= b < B

        def every_batch(eng, batch):
            for b in (-2, -1, 0, 1):
                batch(b, b % 2, b // 2)
            with eng.Fori(1, B // 2 - 2) as i:
                for par in range(2):
                    batch(i * 2 + par, par, i)
            for b in range(B - 4, B + 2):
                batch(b, b % 2, b // 2)

        def parts_in(s, pair):
            return s, 16 * COPIES * (pair + 1)

        def slot(u):
            u %= UNITS
            return slice(u % QB * H + u // QB * HU, u % QB * H + u // QB * HU + HU)

        def some_heads(t, part):
            h0, h1 = NORM_HEADS[part]
            pattern = "p (q h) z -> p q h z" if len(t.shape) == 3 else "p (q h) -> p q h"
            return t[:].rearrange(pattern, q=QB)[:, :, h0:h1]

        @block.sync
        def _(sp):
            def load_wq():
                sp.dma_start(Wq[:, 0:2, 0:C], wq[0:2 * P, :].rearrange("(k p) n -> p k n", p=P)).then_inc(
                    wq_in, 16)
                for half in range(2):
                    sp.dma_start(Wq[ROWS[2] * half:ROWS[2] * (half + 1), 2, 0:C], wq[2 * P:C, :]).then_inc(
                        wq_in, 16)

            def load_other_weights():
                for dst, src, s in ((Wk, wk, wk_in), (ipT, ipt, ip_in), (Wki, wki, ip_in), (Wvi, wvi, ip_in),
                                    (Wv, wv, wvo_in)):
                    src = src if dst is ipT else src.rearrange("(k p) n -> p k n", p=P)
                    sp.dma_start(dst[:], src).then_inc(s, 16)
                sp.dma_start(Wo[:, 0:2, :], wo[0:2 * P, :].rearrange("(k p) n -> p k n", p=P)).then_inc(
                    wvo_in, 16)
                sp.dma_start(Wo[0:ROWS[2], 2, :], wo[2 * P:C, :]).then_inc(wvo_in, 16)
                sp.dma_start(Wo[ROWS[2]:ROWS[2] + 1, 2, :], bo).then_inc(wvo_in, 16)

            def load_batch(b, par):
                sp.dma_start(xT[par][:, 0:2, :], xt01[b]).then_inc(batch_in[par], 16)
                for half in range(2):
                    sp.dma_start(xT[par][ROWS[2] * half:ROWS[2] * (half + 1), 2, :], xt2[b]).then_inc(
                        batch_in[par], 16)
                sp.dma_start(cT[par][:], ctxt[b]).then_inc(batch_in[par], 16)

            def copy_parts(stack, hi, lo, parts, s):
                for r in range(P // QUAD):
                    n = len(range(r, PAIRS, P // QUAD))
                    for i, part in enumerate(parts):
                        src = (hi, lo)[part][QUAD * r:QUAD * (r + 1), 0:n]
                        if len(src.shape) == 4:
                            src = src.rearrange("p m e t -> p m (e t)")
                        sp.dma_start(stack[QUAD * i:QUAD * (i + 1), r:PAIRS:P // QUAD, :].bitcast(f32),
                                     src.bitcast(f32)).then_inc(s, 16)

            load_wq()
            load_batch(0, 0)
            load_other_weights()

            def batch(b, par, pair):
                if is_batch(b + 3):
                    wait(sp, context_split, b + 2)
                    load_batch(b + 3, 1 - par)
                if isinstance(b, int) and b == -1:
                    sp.wait_ge(vip_ready, 1)
                    sp.dma_start(vip_dram.rearrange("b n c -> (b n) c"), vip[:]).then_inc(vip_out, 16)
                    sp.wait_ge(vip_out, 16)
                if is_batch(b):
                    wait(sp, vbd_ready, b - 1)
                    sp.dma_start(viprep[par][:], vip_dram[b].unsqueeze(0).broadcast_to(
                        [H, N_IP, C])).then_inc(vip_in[par], 16)
                    wait(sp, back_free, BACK * (b - 1))
                    sp.dma_start(xn[par][:], x[b].rearrange("(q p) c -> p q c", p=P)).then_inc(
                        xn_in[par], 16)
                if is_batch(b - 2):
                    wait(sp, back_free, BACK * (b - 1))
                    sp.dma_start(out[b - 2].rearrange("(q p) c -> p q c", p=P), y[par][:]).then_inc(
                        stored[par], 16)
                if is_batch(b + 2):
                    sp.wait_ge(kd_ready, b + 3)
                    copy_parts(ks[par], kdhi, kdlo, (0, 1, 0), ks_in[par])
                    sp.wait_ge(q_low, 2 * (b + 3))
                    copy_parts(qs[par], qhi[par], qlo[par], (0, 0, 1), qs_in[par])

            every_batch(sp, batch)
            for par in range(2):
                sp.wait_ge(stored[par], 16 * (B // 2))

        @block.tensor
        def _(pe):
            mm, tr = nc.tensor.matmul, nc.tensor.transpose

            pe.wait_ge(preset, 1)
            pe.wait_ge(w_split, 2)

            def image_prompt():
                pe.wait_ge(ip_in, 16 * 3)
                for m in range(KC):
                    for k in range(KE):
                        last = mm(yP[0][0:ROWS[m], 0, m * P:(m + 1) * P], Wki[:, k, m * P:m * P + ROWS[m]],
                                  ipT[:, k, :], start=k == 0, stop=k == KE - 1)
                last.then_inc(ip_k_mm, 1)
                pe.wait_ge(ip_squared, 1)
                for k in range(KE):
                    last = mm(transP[:, 0:1], ipT2[:, k, :], ones[:, 0:1], start=k == 0, stop=k == KE - 1)
                last.then_inc(ip_norm_mm, 1)
                for k in range(KE):
                    last = mm(scoresP[0][:, 0:C], ipT[:, k, :], Wvi[:, k, :], start=k == 0, stop=k == KE - 1)
                last.then_inc(ip_v_mm, 1)
                pe.wait_ge(ip_diag, 1)
                mm(scoresP[1][:, 0:P], ones[:], diag[:, 0, :], start=True, stop=True).then_inc(ip_spread_mm, 1)

            def units_may_start():
                pe.wait_ge(kip_ready, 1)
                pe.wait_ge(vip_ready, 1)
                pe.wait_ge(ip_inv, 1)
                pe.wait_ge(w_split, 4)

            def products_of(dst, operands):
                for n, (stationary, moving) in enumerate(operands):
                    last = mm(dst, stationary, moving, start=n == 0, stop=n == len(operands) - 1)
                return last

            def kq(b, par, pair, piece):
                if not is_batch(b):
                    return
                if piece == Q01:
                    wait(pe, vg_free, b)
                wait(pe, kq_free, KQ * b + piece)
                if piece != K_TRANSPOSED:
                    pe.wait_ge(context_split if piece == K_ROWS else x_split, b + 1)
                if piece in (Q01, Q2):
                    for m in (0, 1) if piece == Q01 else (2,):
                        cols = slice(m * P, (m + 1) * P)
                        last = products_of(sharedP[:, m % 2 * S:m % 2 * S + S], [
                            (w[:, k, cols], x_[:, k, :]) for k in range(KC - 1)
                            for w, x_ in ((Wqhi, xhi), (Wqlo, xhi), (Wqhi, xlo))] + [
                            (Wqhi[:, KC - 1, cols], x_[:, KC - 1, :]) for x_ in (xhi, xlo)])
                elif piece == K_ROWS:
                    if isinstance(b, int) and b == 0:
                        pe.wait_ge(w_split, 3)
                    last = products_of(sharedP[:, 0:C], [
                        (c[:, k, :], w[:, k, :]) for k in range(KE)
                        for c, w in ((chi, Wkhi), (chi, Wklo), (clo, Wkhi))])
                else:
                    for m in range(KC):
                        last = tr(sharedP[0:ROWS[m], m * T:(m + 1) * T], k_rows[:, m * P:m * P + ROWS[m]],
                                  ident[0:T, 0:T])
                last.then_inc(kq_mm, 1)

            def vg(b, par, pair, piece):
                if not is_batch(b):
                    return
                if isinstance(b, int) and b < 3:
                    pe.wait_ge(kq_free, KQ * (b + 1))
                else:
                    pe.wait_ge(back_free, BACK * (b - 2))
                products_of(sharedP[:, 0:C + P], [
                    (c[:, k, :], w[:, k, :]) for k in range(KE)
                    for c, w in ((chi, vchi), (chi, vclo), (clo, vchi))]).then_inc(vg_mm, 1)

            def back(b, par, pair, piece):
                if not is_batch(b):
                    return
                if piece == 0:
                    if isinstance(b, int):
                        pe.wait_ge(vg_free, min(b + 3, B))
                        pe.wait_ge(kq_free, KQ * min(b + 4, B))
                    else:
                        pe.wait_ge(kq_free, KQ * (b + 4))
                    pe.wait_ge(pip_done, b + 1)
                wait(pe, back_free, BACK * b + piece)
                if piece == 0:
                    for q in range(QB):
                        last = tr(sharedP[0:H * N_IP, q * P:(q + 1) * P], pip[par][:, q, :], ident[:])
                elif piece in (1, 2):
                    if piece == 1:
                        pe.wait_ge(on_done, b + 1)
                        pe.wait_ge(vbd_ready, b + 1)
                    tiles = (0, 1) if piece == 1 else (2,)
                    for m in tiles:
                        mm(sharedP[0:ROWS[m], m % 2 * S:m % 2 * S + S], vbd[par][:, m * P:m * P + ROWS[m]],
                           pipT[:], start=m == tiles[0], stop=False, skip_group_check=True)
                    for m in tiles:
                        for q in range(QB):
                            at = m % 2 * S + q * P
                            last = mm(sharedP[0:ROWS[m], at:at + P], on[par][:, q, m * P:m * P + ROWS[m]],
                                      ident[:], start=False, stop=True, is_transpose=True,
                                      skip_group_check=True)
                else:
                    q = piece - 3
                    rows = [r + (r != P) for r in ROWS]
                    last = products_of(sharedP[:, 0:C], [
                        (o[0:rows[m], m, q * P:(q + 1) * P], w[0:rows[m], m, :]) for m in range(KC)
                        for o, w in ((oThi, Wohi), (oThi, Wolo), (oTlo, Wohi))])
                last.then_inc(back_mm, 1)

            def scores(b, par, pair, u):
                if not is_unit(b, u):
                    return
                g, q = u // QB, u % QB
                if u == 0:
                    pe.wait_ge(*parts_in(qs_in[par], pair))
                    pe.wait_ge(*parts_in(ks_in[par], pair))
                    if isinstance(b, int) and b == 0:
                        pe.wait_ge(stacks_cleared, 1)
                wait(pe, exp_done, UNITS * b + u - 1)
                for j in range(2):
                    last = mm(scoresP[u % 2][:, 2 * T_ALL * j:2 * T_ALL * (j + 1)],
                              qs[par][:, 2 * g + j, q * P:(q + 1) * P], ks[par][:, 2 * g + j, :],
                              start=True, stop=True)
                last.then_inc(scores_mm, 1)

            def transposes(b, par, u):
                if not is_unit(b, u):
                    return
                pe.wait_ge(exp_done, UNITS * b + u + 1)
                wait(pe, probT_ready, UNITS * b + u)
                for h in range(HU):
                    last = tr(transP[0:T, h * P:(h + 1) * P], prob[:, (2 * par + u) % 4, h, :], ident[:])
                last.then_inc(trans_mm, 1)

            def products(b, par, u):
                if not is_unit(b, u):
                    return
                if u == 0:
                    pe.wait_ge(g_spread, b + 1)
                pe.wait_ge(probT_ready, UNITS * b + u + 1)
                wait(pe, zlo_done, UNITS * b + u - 1)
                for h in range(HU):
                    r = h % 2
                    last = mm(yP[u % 2][:, h // 2, r * YW:(r + 1) * YW], probT[:, u % 2, h, :],
                              rhs[par][:, u // QB * 2 + h // 2, r * ZW:r * ZW + YW], start=True, stop=True)
                last.then_inc(y_mm, 1)

            SHARED = [(back, -2, 2), (back, -2, 3), (back, -2, 4), (vg, 1, 0), (kq, 2, Q01),
                      (kq, 2, K_ROWS), (kq, 2, K_TRANSPOSED), (kq, 2, Q2), (back, -1, 0), (back, -1, 1)]

            def batch(b, par, pair):
                for u in range(UNITS):
                    what, off, piece = SHARED[u]
                    what(b + off, (par + off) % 2, pair + (par + off) // 2, piece)
                    if u == 4 and isinstance(b, int) and b == -2:
                        image_prompt()
                    if u == 0 and isinstance(b, int) and b == -1:
                        units_may_start()
                    if u + 2 < UNITS:
                        scores(b, par, pair, u + 2)
                    else:
                        scores(b + 1, 1 - par, pair + par, u + 2 - UNITS)
                    transposes(b, par, u)
                    if u:
                        products(b, par, u - 1)
                    else:
                        products(b - 1, 1 - par, UNITS - 1)

            every_batch(pe, batch)

        @block.scalar
        def _(act):
            copy = nc.scalar.copy
            act.dma_start(ident[:], ident_c).then_inc(consts_in, 16)
            act.dma_start(headmask[:], headmask_c).then_inc(consts_in, 16)
            act.dma_start(ipmask[:], ipmask_c).then_inc(consts_in, 16)
            act.dma_start(smask[:], mask).then_inc(consts_in, 16)

            act.wait_ge(preset, 1)
            act.wait_ge(wq_in, 16 * 3)
            nc.scalar.mul(Wqhi[:], Wq[:], SCALE).then_inc(w_high, 1)

            def wk_high():
                act.wait_ge(wk_in, 16)
                copy(Wkhi[:], Wk[:]).then_inc(w_high, 1)

            def wv_wo_high():
                act.wait_ge(wvo_in, 16 * 4)
                copy(vchi[:, :, 0:C], Wv[:]).then_inc(w_high, 1)
                copy(Wohi[:, 0:2, :], Wo[:, 0:2, :])
                copy(Wohi[0:ROWS[2] + 1, 2, :], Wo[0:ROWS[2] + 1, 2, :]).then_inc(w_high, 1)

            def image_prompt():
                act.wait_ge(ip_k_mm, 1)
                copy(kipT[:, 0:2, :], yP[0][:, 0, 0:2 * P].rearrange("p (m n) -> p m n", m=2))
                copy(kipT[0:ROWS[2], 2, :], yP[0][0:ROWS[2], 0, 2 * P:3 * P]).then_inc(kip_ready, 1)
                act.wait_ge(ip_v_mm, 1)
                copy(vip[:], scoresP[0][:, 0:C]).then_inc(vip_ready, 1)
                act.wait_ge(ip_spread_mm, 1)
                copy(ipinv[:], scoresP[1][:, 0:P]).then_inc(ip_inv, 1)

            def kq(b, par, pair, piece):
                if not is_batch(b):
                    return
                act.wait_ge(kq_mm, KQ * b + piece + 1)
                if piece == Q01:
                    if not isinstance(b, int) or b > 1:
                        act.wait_ge(*parts_in(qs_in[par], pair - 1))
                    q = sharedP[:, 0:2 * S].rearrange("p (m s) -> p m s", m=2)
                    copy(qhi[par][:, 0:2, :], q)
                    copy(qlo[par][:, 0:2, :].bitcast(f32), q).then_inc(kq_free, 1)
                elif piece == Q2:
                    copy(qhi[par][0:ROWS[2], 2, :], sharedP[0:ROWS[2], 0:S])
                    copy(qlo[par][0:ROWS[2], 2, :].bitcast(f32), sharedP[0:ROWS[2], 0:S]).then_inc(kq_free, 1)
                elif piece == K_ROWS:
                    wait(act, kd_ready, b)
                    copy(k_rows, sharedP[0:T, 0:C]).then_inc(kq_free, 1)
                else:
                    for r, m0, m1 in ((P, 0, 2), (ROWS[2], 2, 3)):
                        k = sharedP[0:r, m0 * T:m1 * T].rearrange("p (m t) -> p m t", t=T)
                        copy(khi[0:r, m0:m1], k)
                        last = copy(klo[0:r, m0:m1].bitcast(f32), k)
                    last.then_inc(kq_free, 1)

            def vg(b, par, pair, piece):
                if not is_batch(b):
                    return
                act.wait_ge(vg_mm, b + 1)
                wait(act, y_mm, UNITS * (b - 1))
                copy(rhs[par][:, 0, ZW:YW], sharedP[0:T, C:C + T])
                copy(ip_products[:], sharedP[0:T, C + T:C + T_ALL])
                for r in range(2):
                    at = r * YW + ZW - DH
                    last = copy(rhs[par][:, :, at:at + DH],
                                sharedP[0:T, 0:C].rearrange("p (j r d) -> p r j d", r=2, d=DH)[:, r])
                last.then_inc(vg_free, 1)

            def back(b, par, pair, piece):
                if not is_batch(b):
                    return
                if piece < 3:
                    act.wait_ge(back_mm, BACK * b + piece + 1)
                if piece == 0:
                    copy(pipT[:], sharedP[0:H * N_IP, 0:S]).then_inc(back_free, 1)
                elif piece == 1:
                    copy(oThi[:, 0:2, :], sharedP[:, 0:2 * S].rearrange("p (m s) -> p m s", m=2)
                         ).then_inc(oT_done, 1)
                elif piece == 2:
                    copy(oThi[0:ROWS[2], 2, :], sharedP[0:ROWS[2], 0:S]).then_inc(oT_done, 1)

            def split(b, par, pair, piece):
                if not is_batch(b):
                    return
                if piece == 0:
                    act.wait_ge(batch_in[par], 64 * (pair + 1))
                    wait(act, kq_mm, KQ * b)
                    copy(xhi[:], xT[par][:]).then_inc(split_hi, 1)
                else:
                    wait(act, vg_mm, b)
                    copy(vchi[:, :, C:C + T_ALL], cT[par][:]).then_inc(split_hi, 1)

            def evac_trans(b, par, u):
                if not is_unit(b, u):
                    return
                act.wait_ge(trans_mm, UNITS * b + u + 1)
                wait(act, y_mm, UNITS * b + u - 1)
                copy(probT[:, u % 2, :, :], transP[0:T, :].rearrange("t (h s) -> t h s", h=HU)
                     ).then_inc(probT_ready, 1)

            def exp_unit(b, par, u):
                if not is_unit(b, u):
                    return
                act.wait_ge(max_done, UNITS * b + u + 1)
                wait(act, yp_done, UNITS * b + u - 3)
                if u == 0:
                    wait(act, fused_done, b - 1)
                sc = scoresP[u % 2][:, 0:HU * T_ALL].rearrange("p (h t) -> p h t", h=HU)
                copy(sip[par][:, slot(u), :], sc[:, :, T:T_ALL])
                for h in range(HU):
                    last = nc.scalar.activation(prob[:, (2 * par + u) % 4, h, :], sc[:, h, 0:T], ACT.Exp,
                                                bias=negmax[:, u % 2, h:h + 1])
                last.then_inc(exp_done, 1)

            BANK_FIRST = (0, 8, 9)
            SHARED = [(back, -2, 2), (back, -2, 3), (back, -2, 4), (vg, 1, 0), (kq, 2, Q01),
                      (kq, 2, K_ROWS), (kq, 2, K_TRANSPOSED), (kq, 2, Q2), (back, -1, 0), (back, -1, 1)]

            def batch(b, par, pair):
                for u in range(UNITS):
                    what, off, piece = SHARED[u]
                    if u in BANK_FIRST:
                        what(b + off, (par + off) % 2, pair + (par + off) // 2, piece)
                    if u + 1 < UNITS:
                        exp_unit(b, par, u + 1)
                    else:
                        exp_unit(b + 1, 1 - par, 0)
                    if u not in BANK_FIRST:
                        what(b + off, (par + off) % 2, pair + (par + off) // 2, piece)
                    evac_trans(b, par, u)
                    if u == 6 and is_batch(b - 1):
                        act.wait_ge(fsh_done, b)
                        wait(act, pip_done, b - 1)
                        nc.scalar.activation(fexp[:], fsh[:], ACT.Exp).then_inc(fexp_done, 1)
                    if u in (1, 3):
                        split(b + 2, par, pair + 1, u // 3)
                    if isinstance(b, int) and b == -2:
                        if u == 1:
                            wk_high()
                        if u == 4:
                            image_prompt()
                            wv_wo_high()

            every_batch(act, batch)

        @block.vector
        def _(dve):
            v = nc.vector
            v.memset(ones[:], 1.0)
            v.memset(Wq[:, :, C:CP], 0.0)
            for t in (khi, klo, kipT):
                v.memset(t[ROWS[2]:, 2, :].bitcast(f32), 0.0)
            for t in (vchi, vclo):
                v.memset(t[:, :, C + T_ALL:].bitcast(f32), 0.0)
            for i in range(2):
                for r in range(2):
                    v.memset(rhs[i][:, :, r * YW + N_IP:r * YW + N_IP + 1], 1.0)
                    v.memset(rhs[i][:, :, r * YW + N_IP + 1:r * YW + N_IP + 2], 0.0)
            v.memset(oTlo[ROWS[2]:ROWS[2] + 1, 2, :].bitcast(f32), 0.0)
            v.memset(oThi[ROWS[2]:ROWS[2] + 1, 2, :].bitcast(f32), 1.0).then_inc(preset, 1)
            dve.wait_ge(w_high, 1)
            v.scalar_tensor_tensor(Wqlo[:], Wq[:], SCALE, Wqhi[:].bitcast(f32), ALU.mult,
                                   ALU.subtract).then_inc(w_split, 1)
            dve.wait_ge(w_split, 1)
            low_rows = slice(ROWS[2], P)
            v.tensor_copy(Wqhi[low_rows, 2, :], Wqlo[low_rows, 2, :].bitcast(f32)).then_inc(w_split, 1)

            def one_off_work():
                dve.wait_ge(w_high, 2)
                v.tensor_tensor(Wklo[:], Wk[:], Wkhi[:].bitcast(f32), ALU.subtract).then_inc(w_split, 1)
                dve.wait_ge(ip_in, 16 * 3)
                v.tensor_tensor(ipT2[:], ipT[:], ipT[:], ALU.mult).then_inc(ip_squared, 1)
                dve.wait_ge(ip_norm_mm, 1)
                v.tensor_scalar(ipnorm[:], transP[:, 0:1], EPS * EPS, 1.0 / SEM_SCALE ** 2,
                                ALU.max, ALU.mult).then_inc(ip_floor, 1)
                dve.wait_ge(kip_ready, 1)
                v.tensor_copy(kiphi[:], kipT[:]).then_inc(kip_split, 1)
                dve.wait_ge(kip_split, 1)
                v.tensor_tensor(kiplo[:], kipT[:], kiphi[:].bitcast(f32), ALU.subtract).then_inc(kip_split, 1)
                dve.wait_ge(ip_power, 1)
                dve.wait_ge(consts_in, N_CONSTS)
                v.tensor_scalar(diag[:, 0, :], ident[:], ipnorm[:], None, ALU.mult).then_inc(ip_diag, 1)
                dve.wait_ge(w_high, 4)
                v.tensor_tensor(vclo[:, :, 0:C], Wv[:], vchi[:, :, 0:C].bitcast(f32), ALU.subtract)
                v.tensor_tensor(Wolo[:, 0:2, :], Wo[:, 0:2, :], Wohi[:, 0:2, :].bitcast(f32), ALU.subtract)
                last_rows = slice(0, ROWS[2] + 1)
                v.tensor_tensor(Wolo[last_rows, 2, :], Wo[last_rows, 2, :], Wohi[last_rows, 2, :].bitcast(f32),
                                ALU.subtract).then_inc(w_split, 1)

            def clear_stacks():
                for i in range(2):
                    v.memset(qs[i][PARTS * QUAD:, :, :].bitcast(f32), 0.0)
                    last = v.memset(ks[i][PARTS * QUAD:, :, :].bitcast(f32), 0.0)
                last.then_inc(stacks_cleared, 1)

            def evac_zlo(b, par, u):
                if not is_unit(b, u):
                    return
                if u == 0:
                    wait(dve, on_done, b - 1)
                z = yP[u % 2][:, :, 0:2 * YW]
                for r in range(2):
                    at = r * (YW + T)
                    dst = zlo[par][:, slot(u), :].rearrange("p (k r) z -> p r k z", r=2)[:, r]
                    last = v.tensor_copy(dst, z[:, :, at:at + ZW])
                last.then_inc(zlo_done, 1)

            def row_max(b, par, u):
                if not is_unit(b, u):
                    return
                sc = scoresP[u % 2][:, 0:HU * T_ALL].rearrange("p (h t) -> p h t", h=HU)
                dve.wait_ge(scores_mm, UNITS * b + u + 1)
                wait(dve, exp_done, UNITS * b + u - 1)
                v.tensor_reduce(negmax[:, u % 2, :], sc[:, :, 0:T], AX, ALU.max, negate=True
                                ).then_inc(max_done, 1)

            def y_times_p(b, par, u):
                if not is_unit(b, u):
                    return
                dve.wait_ge(y_mm, UNITS * b + u + 1)
                wait(dve, yp_done, UNITS * b + u)
                if u == 0:
                    wait(dve, norm2c_done, NORMS * (b - 1))
                for h in range(HU):
                    at = ZW + h % 2 * T
                    i = slot(u).start + h
                    last = v.scalar_tensor_tensor(yp[:, h, :], yP[u % 2][:, h // 2, at:at + T], 1.0,
                                                  prob[:, (2 * par + u) % 4, h, :], ALU.mult, ALU.mult,
                                                  accum_out=norm2[par][:, i:i + 1])
                last.then_inc(yp_done, 1)

            def g_blocks(b, par):
                if not is_batch(b):
                    return
                dve.wait_ge(vg_free, b + 1)
                if isinstance(b, int) and b == 0:
                    dve.wait_ge(ip_inv, 1)
                v.tensor_copy(rhs[par][:, 1:, ZW:YW], rhs[par][:, 0:1, ZW:YW].broadcast_to(
                    [T, H // 2 - 1, T]))
                for r in range(2):
                    at = r * YW
                    last = v.tensor_tensor(
                        rhs[par][:, :, at:at + N_IP],
                        ip_products[:].unsqueeze(1).broadcast_to([T, H // 2, N_IP]),
                        ipinv[0:T, bass.ds(b * N_IP, N_IP)].unsqueeze(1).broadcast_to([T, H // 2, N_IP]),
                        ALU.mult)
                last.then_inc(g_spread, 1)

            def split_x(b, par):
                if not is_batch(b):
                    return
                dve.wait_ge(split_hi, 2 * b + 1)
                v.tensor_tensor(xlo[:], xT[par][:], xhi[:].bitcast(f32), ALU.subtract).then_inc(x_split, 1)

            def norms(b, par, part):
                if not is_batch(b):
                    return
                dve.wait_ge(zlo_done, UNITS * b + NORM_HEADS[part][1] // HU * QB)
                l = some_heads(zlo[par], part)[:, :, :, N_IP]
                v.scalar_tensor_tensor(some_heads(floor2, part), l, EPS * EPS, l, ALU.mult,
                                       ALU.mult).then_inc(floor_done, 1)
                wait(dve, on_done, b)
                v.reciprocal(some_heads(rl, part), l).then_inc(rl_done, 1)
                dve.wait_ge(floor_done, NORMS * b + part + 1)
                wait(dve, rnorm_done, NORMS * b)
                v.tensor_tensor(some_heads(norm2c, part), some_heads(norm2[par], part),
                                some_heads(floor2, part), ALU.max).then_inc(norm2c_done, 1)

            def per_head(t):
                return t[:].unsqueeze(2).broadcast_to([P, QB * H, N_IP])

            def ip_scores(b, par):
                if not is_batch(b):
                    return
                dve.wait_ge(rnorm_done, NORMS * (b + 1))
                v.tensor_tensor(cosn[:], zlo[par][:, :, 0:N_IP], per_head(rnorm), ALU.mult).then_inc(cos_done, 1)
                dve.wait_ge(cos_done, b + 1)
                dve.wait_ge(exp_done, UNITS * (b + 1))
                v.tensor_tensor(fused[:], sip[par][:], cosn[:], ALU.add).then_inc(fused_done, 1)
                dve.wait_ge(fused_done, b + 1)
                v.tensor_reduce(fmax[:], fused[:], AX, ALU.max).then_inc(fmax_done, 1)
                dve.wait_ge(fmax_done, b + 1)
                wait(dve, fexp_done, b)
                v.tensor_tensor(fsh[:], fused[:], per_head(fmax), ALU.subtract).then_inc(fsh_done, 1)

            def ip_probs(b, par):
                if not is_batch(b):
                    return
                dve.wait_ge(fexp_done, b + 1)
                v.tensor_reduce(fsum[:], fexp[:], AX, ALU.add).then_inc(fsum_done, 1)
                dve.wait_ge(fsum_done, b + 1)
                v.reciprocal(frec[:], fsum[:]).then_inc(frec_done, 1)
                dve.wait_ge(frec_done, b + 1)
                v.tensor_tensor(fscale[:].rearrange("p (q h) -> p q h", q=QB),
                                frec[:].rearrange("p (q h) -> p q h", q=QB),
                                smask[:].unsqueeze(2).broadcast_to([P, QB, H]), ALU.mult).then_inc(fscale_done, 1)
                dve.wait_ge(fscale_done, b + 1)
                wait(dve, back_mm, BACK * (b - 1))
                v.tensor_tensor(pip[par][:].rearrange("p q (h n) -> p (q h) n", n=N_IP), fexp[:],
                                per_head(fscale), ALU.mult).then_inc(pip_done, 1)

            def low_output(b, piece):
                if not is_batch(b):
                    return
                dve.wait_ge(oT_done, 2 * b + piece)
                if piece == 1:
                    v.tensor_tensor(oTlo[:, 0:2, :], sharedP[:, 0:2 * S].rearrange("p (m s) -> p m s", m=2),
                                    oThi[:, 0:2, :].bitcast(f32), ALU.subtract).then_inc(back_free, 1)
                else:
                    v.tensor_tensor(oTlo[0:ROWS[2], 2, :], sharedP[0:ROWS[2], 0:S],
                                    oThi[0:ROWS[2], 2, :].bitcast(f32), ALU.subtract).then_inc(back_free, 1)

            def output(b, par, pair, q):
                if not is_batch(b):
                    return
                dve.wait_ge(back_mm, BACK * b + 4 + q)
                if q == 0:
                    dve.wait_ge(xn_in[par], 16 * (pair + 1))
                    wait(dve, stored[par], 16 * pair)
                v.tensor_tensor(y[par][:, q, :], sharedP[:, 0:C], xn[par][:, q, :], ALU.add).then_inc(back_free, 1)

            def batch(b, par, pair):
                for u in range(UNITS):
                    if u + 1 < UNITS:
                        row_max(b, par, u + 1)
                    else:
                        row_max(b + 1, 1 - par, 0)
                    if u >= 2:
                        y_times_p(b, par, u - 2)
                        evac_zlo(b, par, u - 2)
                    else:
                        y_times_p(b - 1, 1 - par, u - 2 + UNITS)
                        evac_zlo(b - 1, 1 - par, u - 2 + UNITS)
                    if u == 4:
                        g_blocks(b + 1, 1 - par)
                    if u == 1:
                        norms(b - 1, 1 - par, 1)
                    if u == 8:
                        norms(b, par, 0)
                    if u == 2:
                        split_x(b + 2, par)
                        if isinstance(b, int) and b == -2:
                            one_off_work()
                        if isinstance(b, int) and b == -1:
                            clear_stacks()
                    if u == 9:
                        low_output(b - 1, 1)
                    if u == 0:
                        low_output(b - 2, 2)
                    if u in (1, 2):
                        output(b - 2, par, pair - 1, u - 1)
                    if u == 5:
                        ip_scores(b - 1, 1 - par)
                    if u == 7:
                        ip_probs(b - 1, 1 - par)

            every_batch(dve, batch)

        @block.gpsimd
        def _(pool):
            g = nc.gpsimd
            def spread(dst, k, n):
                return g.tensor_tensor(dst, k.unsqueeze(2).broadcast_to([P, KC, 2, n]),
                                       headmask[:].unsqueeze(1).unsqueeze(3).broadcast_to([P, KC, 2, n]),
                                       ALU.mult)

            g.memset(expo[:], -0.5).then_inc(expo_set, 1)
            pool.wait_ge(expo_set, 1)
            pool.wait_ge(consts_in, N_CONSTS)

            def divide(b, par):
                if not is_batch(b):
                    return
                pool.wait_ge(rl_done, NORMS * (b + 1))
                wait(pool, back_mm, BACK * (b - 1))
                g.tensor_tensor(on[par][:].rearrange("p q (h d) -> p (q h) d", d=DH),
                                zlo[par][:, :, ZW - DH:ZW],
                                rl[:].unsqueeze(2).broadcast_to([P, QB * H, DH]), ALU.mult).then_inc(on_done, 1)

            def split_context(b, par):
                if not is_batch(b):
                    return
                pool.wait_ge(split_hi, 2 * b + 2)
                pool.wait_ge(x_split, b + 1)
                g.tensor_tensor(vclo[:, :, C:C + T_ALL], cT[par][:], vchi[:, :, C:C + T_ALL].bitcast(f32),
                                ALU.subtract).then_inc(context_split, 1)

            def low_q(b, par, piece):
                if not is_batch(b):
                    return
                pool.wait_ge(kq_free, KQ * b + 1 + piece)
                t = (slice(0, P), slice(0, 2)) if piece == Q01 else (slice(0, ROWS[2]), slice(2, 3))
                g.tensor_tensor(qlo[par][t], qlo[par][t].bitcast(f32), qhi[par][t].bitcast(f32),
                                ALU.subtract).then_inc(q_low, 1)

            def k_blocks(b, par, pair):
                if not is_batch(b):
                    return
                pool.wait_ge(kq_free, KQ * b + K_TRANSPOSED + 1)
                g.tensor_tensor(klo[:], klo[:].bitcast(f32), khi[:].bitcast(f32), ALU.subtract).then_inc(k_low, 1)
                if not isinstance(b, int) or b > 0:
                    pool.wait_ge(*parts_in(ks_in[1 - par], pair - 1 + par))
                spread(kdhi[:, :, :, 0:T], khi[:].bitcast(f32), T)
                pool.wait_ge(k_low, b + 1)
                spread(kdlo[:, :, :, 0:T], klo[:].bitcast(f32), T)
                if isinstance(b, int) and b == 0:
                    pool.wait_ge(kdip_ready, 1)
                wait(pool, scores_mm, UNITS * (b - 1))
                cols = bass.ds(b * N_IP, N_IP)
                for m in range(KC):
                    g.tensor_copy(kdhi[:, m, :, T:T_ALL], kdiphi[:, m, :, cols].bitcast(f32))
                    last = g.tensor_copy(kdlo[:, m, :, T:T_ALL], kdiplo[:, m, :, cols].bitcast(f32))
                last.then_inc(kd_ready, 1)

            def vip_blocks(b, par, pair):
                if not is_batch(b):
                    return
                pool.wait_ge(vip_in[par], 16 * (pair + 1))
                wait(pool, back_mm, BACK * (b - 1))
                g.tensor_tensor(vbd[par][:], viprep[par][:], ipmask[:], ALU.mult).then_inc(vbd_ready, 1)

            def inverse_norms(b, part):
                if not is_batch(b):
                    return
                pool.wait_ge(norm2c_done, NORMS * b + part + 1)
                wait(pool, cos_done, b)
                h0, h1 = NORM_HEADS[part]
                g.tensor_tensor(some_heads(rnorm, part), some_heads(norm2c, part),
                                expo[:].unsqueeze(2).broadcast_to([P, QB, h1 - h0]), ALU.pow).then_inc(rnorm_done, 1)

            def batch(b, par, pair):
                for u in range(UNITS):
                    if u == 4:
                        split_context(b + 2, par)
                        if isinstance(b, int) and b == -2:
                            pool.wait_ge(ip_floor, 1)
                            g.tensor_tensor(ipnorm[:], ipnorm[:], expo[:], ALU.pow).then_inc(ip_power, 1)
                    if u == 2:
                        inverse_norms(b - 1, 1)
                    if u == 9:
                        inverse_norms(b, 0)
                    if u == 6:
                        low_q(b + 2, par, Q01)
                        divide(b - 1, 1 - par)
                    if u == 6 and isinstance(b, int) and b == -2:
                        pool.wait_ge(kip_split, 2)
                        spread(kdiphi[:], kiphi[:].bitcast(f32), B * N_IP)
                        spread(kdiplo[:], kiplo[:].bitcast(f32), B * N_IP).then_inc(kdip_ready, 1)
                    if u == 7:
                        k_blocks(b + 2, par, pair + 1)
                    if u == 8:
                        low_q(b + 2, par, Q2)
                    if u == 0:
                        vip_blocks(b - 1, 1 - par, pair - 1 + par)

            every_batch(pool, batch)


def kernel(**inputs):
    import numpy as np
    import concourse.bacc as bacc
    from concourse.bass_utils import run_bass_kernel_spmd

    f = {k: np.asarray(a) for k, a in inputs.items()}
    x, c = f["x"], f["ctx_2048"]
    xt = x.transpose(0, 2, 1)
    ct = c.transpose(0, 2, 1).reshape(B, KE, P, T_ALL)
    ip = c[:, T:, :].reshape(B * N_IP, KE, P)
    heads_of_rows = np.arange(P) // DH
    arrays = {
        "x": x,
        "xt01": xt[:, :2 * P].reshape(B, 2, P, S).transpose(0, 2, 1, 3),
        "xt2": xt[:, 2 * P:],
        "ctxt": ct.transpose(0, 2, 1, 3),
        "ipt": ip.transpose(2, 1, 0),
        "mask": f["fside_S_0"].reshape(QB, P).T,
        "wq": f["L0_xattn_W_q"], "wk": f["L0_xattn_W_k"], "wv": f["L0_xattn_W_v"],
        "wki": f["L0_xattn_W_k_ip"], "wvi": f["L0_xattn_W_v_ip"], "wo": f["L0_xattn_W_out"],
        "bo": f["L0_xattn_b_out"].reshape(1, C),
        "ident": np.eye(P, dtype=np.float32),
        "headmask": (heads_of_rows[:, None] % 2 == np.arange(2)[None]).astype(np.float32),
        "ipmask": (np.arange(H * N_IP)[:, None] // N_IP == np.arange(C)[None] // DH).astype(np.float32),
    }
    nc = bacc.Bacc("TRN2", target_bir_lowering=False, num_devices=1)
    ins, args = {}, []
    for name, a in arrays.items():
        a = np.ascontiguousarray(a)
        ins[f"in_{name}"] = a
        args.append(nc.dram_tensor(f"in_{name}", a.shape, mybir.dt.from_np(a.dtype), kind="ExternalInput").ap())
    args.append(nc.dram_tensor("out_y", (B, S, C), mybir.dt.float32, kind="ExternalOutput").ap())
    cross_attention(nc, *args)
    r = run_bass_kernel_spmd(nc, [ins], core_ids=[0])
    return r.results[0]["out_y"]
```
